# Optimizing a Trainium2 kernel written in Bass

```python
import numpy as np
import jax
import jax.numpy as jnp

def _softmax(x, axis=-1):
    return jax.nn.softmax(x, axis=axis)

def _gelu(x):
    return jax.nn.gelu(x, approximate=True)

def _silu(x):
    return jax.nn.silu(x)

def _sigmoid(x):
    return jax.nn.sigmoid(x)

def _layernorm(x, axis=-1, eps=1e-05):
    m = jnp.mean(x, axis=axis, keepdims=True)
    v = jnp.var(x, axis=axis, keepdims=True)
    return (x - m) / jnp.sqrt(v + eps)

def _scatter_add(tgt, idx, src, axis=0):
    return tgt.at[idx].add(src)

def _segment_sum(src, seg, n):
    return jax.ops.segment_sum(src, seg, n)
kernel_name = 'mk_audio_tower_d1_tok_audfeat256_r4_84e5c6'

def setup_inputs(seed: int=0):
    np.random.seed(seed)
    _w = jnp.asarray

    def _rec_inputs():
        import jax
        import jax.numpy as jnp
        _rk = jax.random.key(seed)
        x = -0.000113617 + 0.99993 * jax.random.normal(jax.random.fold_in(_rk, 1), (32, 256, 64), jnp.float32)
        return x
    x = _rec_inputs()

    def _L0_tok_setup():
        import jax, jax.numpy as jnp
        import numpy as np
        RATIO = 0.8
        key = jax.random.key(seed)
        k1, k2 = jax.random.split(key)
        B, N, D = (16, 5000, 64)
        x = jax.random.normal(k1, (B, N, D), dtype=jnp.float32)
        w = jax.random.normal(k2, (D,), dtype=jnp.float32) * (1.0 / np.sqrt(D))
        b = jnp.zeros((1,), dtype=jnp.float32)
        return {'x': x, 'w': w, 'b': b}
    _L0_tok_all = _L0_tok_setup()
    _L0_tok_in = {k: v for k, v in _L0_tok_all.items() if k in ('w', 'b')}
    del _L0_tok_all

    def _L0_attn_setup():
        import jax, jax.numpy as jnp
        import numpy as np
        import math
        B, S, D = (4, 1024, 64)
        key = jax.random.key(seed)
        ks = jax.random.split(key, 9)
        s = 1.0 / math.sqrt(D)
        return {'src': jax.random.normal(ks[0], (B, S, D), dtype=jnp.float32), 'Wq': jax.random.normal(ks[1], (D, D), dtype=jnp.float32) * s, 'bq': jax.random.normal(ks[2], (D,), dtype=jnp.float32) * s, 'Wk': jax.random.normal(ks[3], (D, D), dtype=jnp.float32) * s, 'bk': jax.random.normal(ks[4], (D,), dtype=jnp.float32) * s, 'Wv': jax.random.normal(ks[5], (D, D), dtype=jnp.float32) * s, 'bv': jax.random.normal(ks[6], (D,), dtype=jnp.float32) * s, 'Wo': jax.random.normal(ks[7], (D, D), dtype=jnp.float32) * s, 'bo': jax.random.normal(ks[8], (D,), dtype=jnp.float32) * s}
    _L0_attn_all = _L0_attn_setup()
    _L0_attn_in = {k: v for k, v in _L0_attn_all.items() if k in ('Wq', 'bq', 'Wk', 'bk', 'Wv', 'bv', 'Wo', 'bo')}
    del _L0_attn_all

    def _L0_ffn_setup():
        import jax, jax.numpy as jnp
        import numpy as np
        E = 8
        K = 2
        D = 64
        H = 128
        DOUT = 64
        EPS = 1e-05
        key = jax.random.key(seed)
        ks = jax.random.split(key, 9)
        s = 0.02
        return {'x': jax.random.normal(ks[0], (4, 2048, D), jnp.float32), 'gamma': 1.0 + 0.05 * jax.random.normal(ks[1], (D,), jnp.float32), 'beta': 0.05 * jax.random.normal(ks[2], (D,), jnp.float32), 'Wr': 0.01 * jax.random.normal(ks[3], (D, E), jnp.float32), 'br': jnp.zeros((E,), jnp.float32), 'W1': s * jax.random.normal(ks[4], (E, D, H), jnp.float32), 'b1': s * jax.random.normal(ks[5], (E, H), jnp.float32), 'W2': s * jax.random.normal(ks[6], (E, H, DOUT), jnp.float32), 'b2': s * jax.random.normal(ks[7], (E, DOUT), jnp.float32)}
    _L0_ffn_all = _L0_ffn_setup()
    _L0_ffn_in = {k: v for k, v in _L0_ffn_all.items() if k in ('gamma', 'beta', 'Wr', 'br', 'W1', 'b1', 'W2', 'b2')}
    del _L0_ffn_all
    return {'x': x, 'L0_tok_w': _L0_tok_in['w'], 'L0_tok_b': _L0_tok_in['b'], 'L0_attn_Wq': _L0_attn_in['Wq'], 'L0_attn_bq': _L0_attn_in['bq'], 'L0_attn_Wk': _L0_attn_in['Wk'], 'L0_attn_bk': _L0_attn_in['bk'], 'L0_attn_Wv': _L0_attn_in['Wv'], 'L0_attn_bv': _L0_attn_in['bv'], 'L0_attn_Wo': _L0_attn_in['Wo'], 'L0_attn_bo': _L0_attn_in['bo'], 'L0_ffn_gamma': _L0_ffn_in['gamma'], 'L0_ffn_beta': _L0_ffn_in['beta'], 'L0_ffn_Wr': _L0_ffn_in['Wr'], 'L0_ffn_br': _L0_ffn_in['br'], 'L0_ffn_W1': _L0_ffn_in['W1'], 'L0_ffn_b1': _L0_ffn_in['b1'], 'L0_ffn_W2': _L0_ffn_in['W2'], 'L0_ffn_b2': _L0_ffn_in['b2']}

def reference(x, L0_tok_w, L0_tok_b, L0_attn_Wq, L0_attn_bq, L0_attn_Wk, L0_attn_bk, L0_attn_Wv, L0_attn_bv, L0_attn_Wo, L0_attn_bo, L0_ffn_gamma, L0_ffn_beta, L0_ffn_Wr, L0_ffn_br, L0_ffn_W1, L0_ffn_b1, L0_ffn_W2, L0_ffn_b2):
    import jax
    import jax.numpy as jnp

    def _L0_tok_ref(x, w, b):
        import jax, jax.numpy as jnp
        import numpy as np
        RATIO = 0.8
        B, N, D = x.shape
        scores = jnp.einsum('bnd,d->bn', x, w) + b[0]
        k = max(1, int(N * RATIO))
        top_scores, top_indices = jax.lax.top_k(scores, k)
        gate = jax.nn.sigmoid(top_scores)[..., None]
        selected = jnp.take_along_axis(x, top_indices[..., None], axis=1)
        return selected * gate

    def _L0_attn_ref(src, Wq, bq, Wk, bk, Wv, bv, Wo, bo):
        import jax, jax.numpy as jnp
        import numpy as np
        import math
        B, S, D = (4, 1024, 64)
        q = src @ Wq.T + bq
        k = src @ Wk.T + bk
        v = src @ Wv.T + bv
        row_mask = (q[:, :, 0] != 0) & (k[:, :, 0] != 0)
        mask = row_mask[:, :, None]
        scale = 1.0 / math.sqrt(D)
        scores = jnp.einsum('bid,bjd->bij', q, k) * scale
        scores = jnp.where(mask, scores, jnp.float32(-1000000000.0))
        prob = jax.nn.softmax(scores, axis=-1)
        prob = jnp.where(mask, prob, 0.0)
        out = jnp.einsum('bij,bjd->bid', prob, v)
        return out @ Wo.T + bo

    def _L0_ffn_ref(x, gamma, beta, Wr, br, W1, b1, W2, b2):
        import jax, jax.numpy as jnp
        import numpy as np
        E = 8
        K = 2
        D = 64
        H = 128
        DOUT = 64
        EPS = 1e-05
        mu = jnp.mean(x, axis=-1, keepdims=True)
        var = jnp.mean(jnp.square(x - mu), axis=-1, keepdims=True)
        xn = (x - mu) * jax.lax.rsqrt(var + EPS) * gamma + beta
        logits = jnp.einsum('bsd,de->bse', xn, Wr) + br
        top_vals, top_idx = jax.lax.top_k(logits, K)
        w = jax.nn.softmax(top_vals, axis=-1)
        w_full = jnp.einsum('bsk,bske->bse', w, jax.nn.one_hot(top_idx, E, dtype=w.dtype))
        y = jnp.zeros(x.shape[:-1] + (DOUT,), x.dtype)
        for e in range(E):
            h = jax.nn.gelu(jnp.einsum('bsd,dh->bsh', xn, W1[e]) + b1[e], approximate=False)
            y_e = jnp.einsum('bsh,hd->bsd', h, W2[e]) + b2[e]
            y = y + y_e * w_full[..., e, None]
        return y
    h = _L0_tok_ref(x, L0_tok_w, L0_tok_b)
    h = h + _L0_attn_ref(_layernorm(h, axis=-1), L0_attn_Wq, L0_attn_bq, L0_attn_Wk, L0_attn_bk, L0_attn_Wv, L0_attn_bv, L0_attn_Wo, L0_attn_bo)
    h = h + _L0_ffn_ref(_layernorm(h, axis=-1), L0_ffn_gamma, L0_ffn_beta, L0_ffn_Wr, L0_ffn_br, L0_ffn_W1, L0_ffn_b1, L0_ffn_W2, L0_ffn_b2)
    return h

_drawn_inputs = setup_inputs


def setup_inputs(seed=0):
    import zlib

    import numpy as np

    out = dict(_drawn_inputs(seed))
    spreads = {'L0_ffn_br': (0.0, 0.1)}
    factors = {'L0_attn_bk': 8.0,
     'L0_ffn_gamma': 8.0,
     'L0_ffn_beta': 8.0,
     'L0_ffn_Wr': 3.774,
     'L0_ffn_W1': 2.903,
     'L0_ffn_b1': 8.0,
     'L0_ffn_W2': 2.864,
     'L0_ffn_b2': 2.745}
    for name, (base, spread) in spreads.items():
        noise = np.random.default_rng([zlib.crc32(name.encode()), seed]).standard_normal(out[name].shape)
        drawn = base * np.exp(spread * noise) if base else spread * noise
        out[name] = jnp.asarray(drawn.astype(out[name].dtype))
    for name, factor in factors.items():
        out[name] = (out[name] * factor).astype(out[name].dtype)
    return out
```

```python
import concourse.bass as bass
from concourse import mybir
from concourse.alu_op_type import AluOpType as ALU
from contextlib import ExitStack


def audio_tower_kernel(
    nc: bass.Bass,
    x: bass.AP,
    tok_w: bass.AP,
    tok_b: bass.AP,
    Wq: bass.AP,
    bq: bass.AP,
    Wk: bass.AP,
    bk: bass.AP,
    Wv: bass.AP,
    bv: bass.AP,
    Wo: bass.AP,
    bo: bass.AP,
    gamma: bass.AP,
    beta: bass.AP,
    Wr: bass.AP,
    br: bass.AP,
    W1: bass.AP,
    b1: bass.AP,
    W2: bass.AP,
    b2: bass.AP,
    out: bass.AP,
):
    fp32 = mybir.dt.float32
    fp32r = mybir.dt.float32r
    bf16 = mybir.dt.bfloat16
    i32 = mybir.dt.int32
    ACT = mybir.ActivationFunctionType
    AX = mybir.AxisListType

    B, N, D = x.shape
    S = out.shape[1]
    P = 128
    T = N // P
    R = 2
    Q = S // R
    NE, HID = W1.shape[0], W1.shape[2]
    PAIRS = B // 2
    UNITS = PAIRS // 2
    TT = 2 * T
    G = 2 * R
    C = 2 * S
    VX = D + 2
    SCALE = float(D) ** -0.5
    EPS = 1e-5

    x_tiles = x.rearrange("b (t p) d -> p (b t) d", p=P)
    h_sorted = nc.dram_tensor("h_sorted", (B * N, D), fp32).ap()
    h_rows = h_sorted.rearrange("(b n) d -> b n d", b=B)[:, 0:S, :].rearrange("b (p r) d -> p b (r d)", r=R)
    out_rows = out.rearrange("b (p r) d -> p b (r d)", r=R)

    ctx = ExitStack()
    with ctx:
        def sb(name, shape, dt=fp32):
            return ctx.enter_context(nc.sbuf_tensor(name, shape, dt))

        def sem(name):
            return ctx.enter_context(nc.semaphore(name))

        ident = sb("ident", [P, P])
        later = sb("later", [P, T * P])
        ones_bf = sb("ones_bf", [P, 1], bf16)
        position = sb("position", [P, S])
        index = sb("index", [P, TT])
        row_index = sb("row_index", [P, B * T])
        neg_half = sb("neg_half", [P, 2 * G])
        falling = sb("falling", [Q, NE])
        w_bc = sb("w_bc", [P, D])
        b_col = sb("b_col", [P, 1])
        bo_bc = sb("bo_bc", [P, D])
        wqk_nat = sb("wqk_nat", [D, 4, D])
        wv_nat = sb("wv_nat", [D, 2, D])
        wo_nat = sb("wo_nat", [D, D])
        woT = sb("woT", [D, D])
        bqk_col = sb("bqk_col", [P, 1])
        bv_col = sb("bv_col", [D, 1])
        wqk_hi = sb("wqk_hi", [P, 2 * D], fp32r)
        wqk_lo = sb("wqk_lo", [P, 2 * D], fp32r)
        wvx_hi = sb("wvx_hi", [P, VX], fp32r)
        wvx_lo = sb("wvx_lo", [P, VX], fp32r)
        vbias = sb("vbias", [Q, VX])
        gamma_col = sb("gamma_col", [P, 1])
        beta_col = sb("beta_col", [D, 1])
        wr_raw = sb("wr_raw", [P, 2, NE])
        wr_g = sb("wr_g", [P, NE])
        wr_hi = sb("wr_hi", [P, 2, 2 * NE], fp32r)
        wr_lo = sb("wr_lo", [P, 2, 2 * NE], fp32r)
        br_col = sb("br_col", [2 * NE, 1])
        br_eff = sb("br_eff", [2 * NE, 1])
        w1_raw = sb("w1_raw", [P, NE, HID])
        w1_g = sb("w1_g", [P, NE, HID])
        w1_hi = sb("w1_hi", [P, NE, HID], fp32r)
        w1_lo = sb("w1_lo", [P, NE, HID], fp32r)
        b1_nat = sb("b1_nat", [NE, HID])
        b1_T = sb("b1_T", [HID, NE])
        b1_eff = sb("b1_eff", [HID, NE])
        w2_sb = sb("w2_sb", [HID, NE, D])
        b2_nat = sb("b2_nat", [NE, 2 * D])
        b2_col = sb("b2_col", [P, NE])
        pick = sb("pick", [P, NE, 2, D])
        spread = sb("spread", [P, NE, P], fp32r)

        X = sb("X", [P, B * T, D])
        H1 = sb("H1", [Q, PAIRS, G * D])
        xw = sb("xw", [P, TT * D])
        ssum = sb("ssum", [P, TT])
        score = [sb(f"score{i}", [P, TT]) for i in range(2)]
        expneg = sb("expneg", [P, TT])
        gate1 = sb("gate1", [P, TT])
        gate = sb("gate", [P, TT])
        h = [sb(f"h{i}", [P, TT, D]) for i in range(2)]
        hb = [sb(f"hb{i}", [P, TT, D]) for i in range(2)]
        hsum = sb("hsum", [P, TT])
        hmean = sb("hmean", [P, TT])
        hc = sb("hc", [P, TT, D])
        sq = sb("sq", [P, TT, D])
        sqsum = sb("sqsum", [P, TT])
        hvar = sb("hvar", [P, TT])
        rstd = sb("rstd", [P, TT])
        z = sb("z", [P, TT, D])
        zsplit = [sb(f"zsplit{i}", [P, TT, 2, D], fp32r) for i in range(2)]
        greater = sb("greater", [P, 2, (T + 1) * P], bf16)
        rowsum = sb("rowsum", [P, TT])
        ahead = sb("ahead", [P, TT])
        rank = sb("rank", [P, TT])
        row_of = [sb(f"row_of{i}", [P, TT], i32) for i in range(2)]
        onehot = [sb(f"onehot{i}", [P, TT, S], fp32r) for i in range(2)]
        zT = [sb(f"zT{i}", [P, C], fp32r) for i in range(2)]
        qk = [sb(f"qk{i}", [P, C]) for i in range(2)]
        k0 = [sb(f"k0_{i}", [P, C]) for i in range(2)]
        v = [sb(f"v{i}", [Q, G, VX]) for i in range(2)]
        smax = sb("smax", [Q, G])
        nmax = [sb(f"nmax{i}", [Q, G]) for i in range(2)]
        E = [sb(f"E{i}", [Q, G, S]) for i in range(2)]
        den = [sb(f"den{i}", [Q, G]) for i in range(2)]
        ET = [sb(f"ET{i}", [Q, R * S]) for i in range(2)]
        OT = sb("OT", [P, S])
        rden = sb("rden", [Q, G])
        rden_q = sb("rden_q", [Q, G])
        rden_qk = sb("rden_qk", [Q, G])
        attn = sb("attn", [Q, 2, R, D])

        TU = 2 * G
        usum = sb("usum", [Q, TU])
        umean = sb("umean", [Q, TU])
        uc = sb("uc", [Q, TU, D])
        usq = sb("usq", [Q, TU, D])
        usqsum = sb("usqsum", [Q, TU])
        uvar = sb("uvar", [Q, TU])
        urstd = sb("urstd", [Q, TU])
        uz = sb("uz", [Q, TU, D])
        usplit = sb("usplit", [Q, TU, 2, D], fp32r)
        uT = [[sb(f"uT{i}_{c}", [P, C], fp32r) for c in range(2)] for i in range(2)]
        lgT = sb("lgT", [2 * NE, C])
        lg = sb("lg", [Q, TU, NE])
        top1 = sb("top1", [Q, TU])
        is1 = sb("is1", [Q, TU, NE])
        pr1 = sb("pr1", [Q, TU, NE])
        pm1 = sb("pm1", [Q, TU])
        sel1 = sb("sel1", [Q, TU, NE])
        lg2 = sb("lg2", [Q, TU, NE])
        top2 = sb("top2", [Q, TU])
        is2 = sb("is2", [Q, TU, NE])
        pr2 = sb("pr2", [Q, TU, NE])
        pm2 = sb("pm2", [Q, TU])
        sel2 = sb("sel2", [Q, TU, NE])
        gap = sb("gap", [Q, TU])
        tanh = sb("tanh", [Q, TU])
        wt1 = sb("wt1", [Q, TU])
        wt2 = sb("wt2", [Q, TU])
        mix1 = sb("mix1", [Q, TU, NE])
        mix2 = sb("mix2", [Q, TU, NE])
        mix = sb("mix", [Q, TU, NE])
        msplit = sb("msplit", [Q, G, 2, 2, NE], fp32r)
        mT = [sb(f"mT{i}", [P, C], fp32r) for i in range(2)]
        hid = [[sb(f"hid{i}_{c}", [HID, C]) for c in range(2)] for i in range(2)]
        mb = [sb(f"mb{i}", [P, C]) for i in range(2)]
        ye = [sb(f"ye{i}", [P, C]) for i in range(2)]
        acc = [sb(f"acc{i}", [P, C]) for i in range(2)]
        y = sb("y", [Q, PAIRS, G, D])

        PS = [ctx.enter_context(nc.psum_tensor(f"PS{i}", [P, 512], fp32)) for i in range(8)]
        srow = PS[0]
        zT_ps, csum_ps = PS[1][:, 0:C], PS[1][:, C:C + TT]
        qk_ps = PS[2][:, 0:C]
        v_ps = PS[3][0:Q, 0:G * VX]
        S_ps = [PS[4], PS[5]]
        ET_ps = [PS[6], PS[7]]
        OT_ps = PS[6][:, 0:S]
        back_ps = PS[7][0:Q, 0:R * P]
        hid_ps = [[PS[0], PS[1]], [PS[2], PS[3]]]
        y_ps = [PS[4], PS[5]]
        mb_ps = PS[6]
        aux_ps = PS[7]

        x_in = [sem(f"x_in{i}") for i in range(4)]
        cst_in, attn_in, ffn_in, w1_in = sem("cst_in"), sem("attn_in"), sem("ffn_in"), sem("w1_in")
        N_CST, N_ATTN, N_FFN, N_W1 = 3, 12, 12, 2
        pool_prep, pool_cst, pe_prep, act_prep, dve_prep = (
            sem("pool_prep"), sem("pool_cst"), sem("pe_prep"), sem("act_prep"), sem("dve_prep"))
        PRE = 13
        pre = sem("pre")
        expneg_ok, sq_ok, rstd_ok, zhi_ok = sem("expneg_ok"), sem("sq_ok"), sem("rstd_ok"), sem("zhi_ok")
        srow_ok = sem("srow_ok")
        CMP = TT
        cmp_ok = sem("cmp_ok")
        csum_ok = sem("csum_ok")
        RANK = 3 + TT
        ranked = sem("ranked")
        scattered = [sem(f"scattered{i}") for i in range(2)]
        h0_in = [sem(f"h0_in{i}") for i in range(2)]
        hb_ok = sem("hb_ok")
        gathered, zT_ok = sem("gathered"), sem("zT_ok")
        qkv_ok, qk_ok, k0_ok, v_ok = sem("qkv_ok"), sem("qk_ok"), sem("k0_ok"), sem("v_ok")
        S_ok, max_ok, exp_ok = sem("S_ok"), sem("max_ok"), sem("exp_ok")
        MAX = 3
        ETp_ok, ET_ok, OTp_ok, OT_ok, back_ok = (
            sem("ETp_ok"), sem("ET_ok"), sem("OTp_ok"), sem("OT_ok"), sem("back_ok"))
        FIN = 5
        h1_ok = sem("h1_ok")
        LN = 7
        ln, usq_ok, urstd_ok, uhi_ok = sem("ln"), sem("usq_ok"), sem("urstd_ok"), sem("uhi_ok")
        uTp_ok, uT_ok = sem("uTp_ok"), sem("uT_ok")
        lgTp_ok, lgT_ok, lgp_ok = sem("lgTp_ok"), sem("lgT_ok"), sem("lgp_ok")
        TOP = 20
        top, tanh_ok = sem("top"), sem("tanh_ok")
        mTp_ok, mT_ok = sem("mTp_ok"), sem("mT_ok")
        mbp_ok, mb_ok = sem("mbp_ok"), sem("mb_ok")
        hidp_ok, hid_ok, yp_ok, ye_ok, acc_ok = (
            sem("hidp_ok"), sem("hid_ok"), sem("yp_ok"), sem("ye_ok"), sem("acc_ok"))
        backB_ok, y_ok = sem("backB_ok"), sem("y_ok")
        stored = sem("stored")

        block = ctx.enter_context(nc.Block())

        def item(half, j, lag, count):
            m = half + (j - lag) // 2
            n = 2 * half + (j - lag)
            if isinstance(half, int) and not 0 <= n < count:
                return None
            return n, m, (j - lag) % 2

        A_LAG, B_LAG = 4, 3

        def run_a(eng, step):
            for s in range(A_LAG + 2):
                step(s // 2, s % 2)
            with eng.Fori(A_LAG // 2 + 1, PAIRS // 2) as half:
                step(half, 0)
                step(half, 1)
            for s in range(PAIRS, PAIRS + A_LAG):
                step(s // 2, s % 2)

        def run_b(eng, step):
            for s in range(B_LAG + 1):
                step(s // 2, s % 2)
            with eng.Fori((B_LAG + 1) // 2, UNITS // 2) as half:
                step(half, 0)
                step(half, 1)
            for s in range(UNITS, UNITS + B_LAG):
                step(s // 2, s % 2)

        def first(n, k=1):
            return isinstance(n, int) and n < k

        @block.sync
        def _(sp):
            cuts = [0, 1, 2, 4, PAIRS]
            sp.dma_start(X[:, 0:TT, :], x_tiles[:, 0:TT, :]).then_inc(x_in[0], 16)
            sp.dma_start(w_bc[:, :], tok_w.partition_broadcast(P)).then_inc(cst_in, 16)
            sp.dma_start(b_col[:, :], tok_b.partition_broadcast(P)).then_inc(cst_in, 16)
            sp.dma_start(bo_bc[:, :], bo.partition_broadcast(P)).then_inc(cst_in, 16)
            for i in (1, 2):
                a, b = TT * cuts[i], TT * cuts[i + 1]
                sp.dma_start(X[:, a:b, :], x_tiles[:, a:b, :]).then_inc(x_in[i], 16)
            for i in range(2):
                sp.dma_start(wqk_nat[:, i, :], Wq).then_inc(attn_in, 16)
                sp.dma_start(wqk_nat[:, 2 + i, :], Wk).then_inc(attn_in, 16)
                sp.dma_start(wv_nat[:, i, :], Wv).then_inc(attn_in, 16)
            sp.dma_start(wo_nat[:, :], Wo).then_inc(attn_in, 16)
            sp.dma_start(bqk_col[0:D, :], bq.unsqueeze(1)).then_inc(attn_in, 16)
            sp.dma_start(bqk_col[D:P, :], bk.unsqueeze(1)).then_inc(attn_in, 16)
            sp.dma_start(bv_col[:, :], bv.unsqueeze(1)).then_inc(attn_in, 16)
            sp.dma_start(vbias[:, D:D + 1], bq[0:1].partition_broadcast(Q)).then_inc(attn_in, 16)
            sp.dma_start(vbias[:, D + 1:VX], bk[0:1].partition_broadcast(Q)).then_inc(attn_in, 16)
            a, b = TT * cuts[3], TT * cuts[4]
            sp.dma_start(X[:, a:b, :], x_tiles[:, a:b, :]).then_inc(x_in[3], 16)
            for i in range(2):
                rows = slice(i * D, (i + 1) * D)
                sp.dma_start(gamma_col[rows, :], gamma.unsqueeze(1)).then_inc(ffn_in, 16)
                sp.dma_start(wr_raw[rows, 0, :], Wr).then_inc(ffn_in, 16)
                sp.dma_start(wr_raw[rows, 1, :], Wr).then_inc(ffn_in, 16)
                sp.dma_start(br_col[i * NE:(i + 1) * NE, :], br.unsqueeze(1)).then_inc(ffn_in, 16)
                sp.dma_start(b2_nat[:, i * D:(i + 1) * D], b2).then_inc(ffn_in, 16)
                sp.dma_start(w1_raw[rows, :, :], W1.rearrange("e d h -> d e h")).then_inc(w1_in, 16)
            sp.dma_start(beta_col[:, :], beta.unsqueeze(1)).then_inc(ffn_in, 16)
            sp.dma_start(b1_nat[:, :], b1).then_inc(ffn_in, 16)
            sp.dma_start(w2_sb[:, :, :], W2.rearrange("e h d -> h e d")).then_inc(w1_in, 16)

            def step_a(half, j):
                it = item(half, j, 2, PAIRS)
                if it:
                    n, m, i = it
                    sp.wait_ge(scattered[i], 16 * TT * (m + 1))
                    sp.dma_start(H1[:, bass.ds(n, 1), :].rearrange("p a (b f) -> p (a b) f", b=2),
                                 h_rows[:, bass.ds(2 * n, 2), :]).then_inc(h0_in[i], 16)

            run_a(sp, step_a)

            def step_b(half, j):
                it = item(half, j, 3, UNITS)
                if it:
                    n, m, i = it
                    sp.wait_ge(y_ok, n + 1)
                    sp.dma_start(out_rows[:, bass.ds(4 * n, 4), :],
                                 y[:, bass.ds(2 * n, 2), :, :].rearrange("p c (b r) d -> p (c b) (r d)", r=R))\
                        .then_inc(stored, 16)

            run_b(sp, step_b)
            sp.wait_ge(stored, 16 * UNITS)

        @block.gpsimd
        def _(pool):
            pool.memset(ident[:, :], 0.0).then_inc(pool_prep, 1)
            pool.memset(later[:, :], 1.0).then_inc(pool_prep, 1)
            pool.memset(ones_bf[:, :], 1.0).then_inc(pool_prep, 1)
            pool.memset(neg_half[:, :], -0.5).then_inc(pool_prep, 1)
            pool.wait_ge(pool_prep, 4)
            pool.affine_select(out=ident[:, :], in_=ident[:, :], compare_op=ALU.not_equal, fill=1.0,
                               base=0, pattern=[[-1, P]], channel_multiplier=1).then_inc(pool_prep, 1)
            pool.affine_select(out=later[:, :], in_=later[:, :], compare_op=ALU.is_gt, fill=0.0,
                               base=0, pattern=[[1, T * P]], channel_multiplier=-1).then_inc(pool_prep, 1)
            pool.iota(position[:, :], pattern=[[1, R], [R, Q]], base=0, channel_multiplier=0,
                      allow_small_or_imprecise_dtypes=True).then_inc(pool_prep, 1)
            pool.iota(index[:, :], pattern=[[0, 2], [P, T]], base=0, channel_multiplier=1,
                      allow_small_or_imprecise_dtypes=True).then_inc(pool_prep, 1)
            pool.iota(row_index[:, :], pattern=[[N, B], [P, T]], base=0, channel_multiplier=1,
                      allow_small_or_imprecise_dtypes=True).then_inc(pool_prep, 1)
            pool.iota(falling[:, :], pattern=[[-1, NE]], base=NE, channel_multiplier=0,
                      allow_small_or_imprecise_dtypes=True).then_inc(pool_prep, 1)
            for i in range(2):
                pool.memset(k0[i][:, :], 0.0).then_inc(pool_prep, 1)
                pool.memset(mT[i][:, :].bitcast(fp32), 0.0).then_inc(pool_prep, 1)
            pool.memset(wr_hi[:, :, :].bitcast(fp32), 0.0).then_inc(pool_prep, 1)
            pool.memset(wr_lo[:, :, :].bitcast(fp32), 0.0).then_inc(pool_prep, 1)
            pool.memset(pick[:, :, :, :], 0.0).then_inc(pool_prep, 1)
            pool.wait_ge(pool_prep, POOL_PREP - 2)
            for part in range(2):
                pool.affine_select(out=pick[:, :, :, :], in_=pick[:, :, :, :], compare_op=ALU.not_equal,
                                   fill=1.0, base=-2 * NE * part, pattern=[[-1, NE], [-NE, 2], [0, D]],
                                   channel_multiplier=1).then_inc(pool_prep, 1)
                pool.wait_ge(pool_prep, POOL_PREP - 1 + part)

            pool.wait_ge(cst_in, 16 * N_CST)

            def step_a(half, j):
                send = item(half, j, 1, PAIRS)
                if send:
                    pool.wait_ge(ranked, RANK * send[0] + 3)
                    pool.wait_ge(hb_ok, send[0] + 1)
                    if not first(send[0], 2):
                        pool.wait_ge(h0_in[send[2]], 16 * send[1])
                it = item(half, j, 0, PAIRS)
                if it:
                    n, m, i = it
                    pool.wait_ge(pre, PRE * n + 6)
                    if not first(n, 2):
                        pool.wait_ge(scattered[i], 16 * TT * m)
                    pool.tensor_tensor(hb[i][:, :, :], h[i][:, :, :], bo_bc[:, None, :].to_broadcast([P, TT, D]),
                                       ALU.add).then_inc(hb_ok, 1)
                    pool.wait_ge(pre, PRE * n + 11)
                    pool.tensor_tensor(rstd[:, :], hvar[:, :], neg_half[:, 0:TT], ALU.pow).then_inc(rstd_ok, 1)
                if send:
                    n, m, i = send
                    for t in range(TT):
                        pool.indirect_dma_start(
                            out=h_sorted[:, :],
                            out_offset=bass.IndirectOffsetOnAxis(ap=row_of[i][:, t:t + 1], axis=0),
                            in_=hb[i][:, t, :], in_offset=None).then_inc(scattered[i], 16)

            run_a(pool, step_a)

            def step_b(half, j):
                norm_, main = item(half, j, 0, UNITS), item(half, j, 2, UNITS)
                for e in range(1, NE):
                    if main:
                        n, m, i = main
                        pool.wait_ge(ye_ok, NE * n + e + 1)
                        if e > 1:
                            pool.wait_ge(acc_ok, (NE - 1) * n + e - 1)
                        pool.tensor_tensor(acc[i][:, :], acc[i][:, :], ye[e % 2][:, :], ALU.add)\
                            .then_inc(acc_ok, 1)
                    if norm_ and e == 6:
                        pool.wait_ge(ln, LN * norm_[0] + 5)
                        pool.tensor_tensor(urstd[:, :], uvar[:, :], neg_half[0:Q, 0:TU], ALU.pow)\
                            .then_inc(urstd_ok, 1)

            run_b(pool, step_b)

        @block.scalar
        def _(act):
            act.wait_ge(pe_prep, 1)
            act.activation(wqk_hi[:, :], PS[0][:, 0:2 * D], ACT.Copy).then_inc(act_prep, 1)
            act.activation(woT[:, :], PS[1][0:D, 0:D], ACT.Copy).then_inc(act_prep, 1)
            act.wait_ge(pe_prep, 2)
            act.activation(wvx_hi[:, 0:D], PS[2][:, 0:D], ACT.Copy).then_inc(act_prep, 1)
            act.activation(wvx_hi[:, D:VX], PS[0][:, 0:D + 1:D], ACT.Copy).then_inc(act_prep, 1)
            act.activation(vbias[:, 0:D], PS[2][0:Q, D:2 * D], ACT.Copy).then_inc(act_prep, 1)
            act.wait_ge(dve_prep, 5)
            act.activation(w1_hi[:, :, :], w1_g[:, :, :], ACT.Copy).then_inc(act_prep, 1)
            act.wait_ge(pool_prep, POOL_PREP)
            for c in range(2):
                act.activation(wr_hi[:, c, NE * c:NE * (c + 1)], wr_g[:, :], ACT.Copy).then_inc(act_prep, 1)
            act.activation(spread[:, :, :], pick[:, :, :, :].rearrange("p e c d -> p e (c d)"), ACT.Copy)\
                .then_inc(act_prep, 1)

            def step_a(half, j):
                it = item(half, j, 4, PAIRS)
                if it:
                    n, m, i = it
                    for b in range(2):
                        act.wait_ge(ETp_ok, 2 * n + b + 1)
                        if not first(n):
                            act.wait_ge(OTp_ok, n)
                        act.activation(ET[b][:, :], ET_ps[b][0:Q, 0:R * S], ACT.Copy).then_inc(ET_ok, 1)
                it = item(half, j, 0, PAIRS)
                if it:
                    n, m, i = it
                    act.wait_ge(pre, PRE * n + 3)
                    act.activation(expneg[:, :], score[i][:, :], ACT.Exp, scale=-1.0).then_inc(expneg_ok, 1)
                it = item(half, j, 2, PAIRS)
                if it:
                    n, m, i = it
                    act.wait_ge(gathered, n + 1)
                    if not first(n, 2):
                        act.wait_ge(qkv_ok, n - 1)
                    act.activation(zT[i][:, :], zT_ps, ACT.Copy).then_inc(zT_ok, 1)
                it = item(half, j, 3, PAIRS)
                if it:
                    n, m, i = it
                    act.wait_ge(max_ok, MAX * (n + 1))
                    if not first(n, 2):
                        act.wait_ge(ETp_ok, 2 * (n - 1))
                        act.wait_ge(h1_ok, FIN * (n - 1))
                    for g in range(G):
                        last = act.activation(E[i][:, g, :], S_ps[g // R][0:Q, (g % R) * S:(g % R + 1) * S],
                                              ACT.Exp, bias=nmax[i][:, g:g + 1], scale=SCALE,
                                              accum_out=den[i][:, g:g + 1])
                    last.then_inc(exp_ok, 1)
                it = item(half, j, 0, PAIRS)
                if it:
                    n, m, i = it
                    act.wait_ge(pre, PRE * n + 9)
                    act.activation(sq[:, :, :], hc[:, :, :], ACT.Square).then_inc(sq_ok, 1)
                it = item(half, j, 2, PAIRS)
                if it:
                    n, m, i = it
                    act.wait_ge(qkv_ok, n + 1)
                    if not first(n, 2):
                        act.wait_ge(S_ok, 2 * (n - 1))
                        act.wait_ge(k0_ok, n - 1)
                    act.activation(qk[i][:, :], qk_ps, ACT.Identity, bias=bqk_col[:, 0:1]).then_inc(qk_ok, 1)
                it = item(half, j, 4, PAIRS)
                if it:
                    n, m, i = it
                    act.wait_ge(OTp_ok, n + 1)
                    if not first(n):
                        act.wait_ge(back_ok, n)
                    act.activation(OT[:, :], OT_ps, ACT.Copy).then_inc(OT_ok, 1)
                it = item(half, j, 0, PAIRS)
                if it:
                    n, m, i = it
                    act.wait_ge(pre, PRE * n + 12)
                    if not first(n, 2):
                        act.wait_ge(gathered, n - 1)
                    act.activation(zsplit[i][:, :, 0, :], z[:, :, :], ACT.Copy).then_inc(zhi_ok, 1)

            run_a(act, step_a)

            def ln_act(it):
                n, m, i = it
                act.wait_ge(ln, LN * n + 3)
                act.activation(usq[:, :, :], uc[:, :, :], ACT.Square).then_inc(usq_ok, 1)
                act.wait_ge(ln, LN * n + 6)
                if not first(n):
                    act.wait_ge(uTp_ok, 2 * n)
                act.activation(usplit[:, :, 0, :], uz[:, :, :], ACT.Copy).then_inc(uhi_ok, 1)

            def step_b(half, j):
                nxt, prep, main = (item(half, j, lag, UNITS) for lag in range(3))
                for e in range(NE):
                    if main:
                        n, m, i = main
                        k = NE * n + e
                        act.wait_ge(mbp_ok, k + 1)
                        if not first(n) or e >= 2:
                            act.wait_ge(ye_ok, k - 1)
                        act.activation(mb[e % 2][:, :], mb_ps[:, 0:C], ACT.Copy).then_inc(mb_ok, 1)
                        for c in range(2):
                            act.wait_ge(hidp_ok, 2 * k + c + 1)
                            if not first(n) or e >= 2:
                                act.wait_ge(yp_ok, k - 1)
                            act.activation(hid[e % 2][c][:, :], hid_ps[e % 2][c][:, 0:C], ACT.Gelu,
                                           bias=b1_eff[:, e:e + 1]).then_inc(hid_ok, 1)
                    if prep and e < 2:
                        n, m, i = prep
                        act.wait_ge(uTp_ok, 2 * n + e + 1)
                        act.activation(uT[i][e][:, :], aux_ps[:, 0:C], ACT.Copy).then_inc(uT_ok, 1)
                    if prep and e == 3:
                        n, m, i = prep
                        act.wait_ge(lgTp_ok, n + 1)
                        act.activation(lgT[:, :], aux_ps[0:2 * NE, 0:C], ACT.Identity,
                                       bias=br_eff[:, 0:1]).then_inc(lgT_ok, 1)
                    if prep and e == 5:
                        n, m, i = prep
                        act.wait_ge(top, TOP * n + 12)
                        act.activation(tanh[:, :], gap[:, :], ACT.Tanh, scale=0.5).then_inc(tanh_ok, 1)
                    if nxt and e == 6:
                        ln_act(nxt)
                    if prep and e == 7:
                        n, m, i = prep
                        act.wait_ge(mTp_ok, n + 1)
                        act.activation(mT[i][0:4 * NE, :], aux_ps[0:4 * NE, 0:C], ACT.Copy).then_inc(mT_ok, 1)

            run_b(act, step_b)

        @block.tensor
        def _(pe):
            pe.wait_ge(pool_prep, 5)
            pe.wait_ge(attn_in, 16 * N_ATTN)
            pe.transpose(PS[0][:, 0:D], wqk_nat[:, 0:2, :].rearrange("o c d -> o (c d)"), ident[0:D, 0:D])
            pe.transpose(PS[0][:, D:2 * D], wqk_nat[:, 2:4, :].rearrange("o c d -> o (c d)"), ident[0:D, 0:D])
            pe.transpose(PS[1][0:D, 0:D], wo_nat[:, :], ident[0:D, 0:D]).then_inc(pe_prep, 1)
            pe.wait_ge(act_prep, 2)
            pe.matmul(PS[2][:, 0:D], wv_nat[:, :, :].rearrange("o c d -> o (c d)"), woT[:, :], start=True, stop=True)
            pe.matmul(PS[2][0:Q, D:2 * D], bv_col[:, 0:1].to_broadcast([D, Q]), woT[:, :],
                      start=True, stop=True).then_inc(pe_prep, 1)
            pe.wait_ge(ffn_in, 16 * N_FFN)
            pe.wait_ge(w1_in, 16 * (N_W1 + 1))
            for e in range(NE):
                pe.matmul(PS[3][:, e:e + 1], w1_raw[0:D, e, :], beta_col[:, :], start=True, stop=True)
            pe.matmul(PS[3][0:2 * NE, 32:33], wr_raw[0:D, :, :].rearrange("d c e -> d (c e)"), beta_col[:, :],
                      start=True, stop=True)
            pe.transpose(PS[3][:, NE:2 * NE], b1_nat[:, :], ident[0:NE, 0:NE])
            pe.transpose(PS[3][:, 2 * NE:3 * NE], b2_nat[:, :], ident[0:NE, 0:NE]).then_inc(pe_prep, 1)
            pe.wait_ge(act_prep, 5)
            pe.wait_ge(dve_prep, DVE_PREP_PSUM)

            def step_a(half, j):
                it = item(half, j, 1, PAIRS)
                if it:
                    n, m, i = it
                    pe.wait_ge(pre, PRE * n + 3)
                    if not first(n):
                        pe.wait_ge(cmp_ok, CMP * n)
                    for t in range(TT):
                        last = pe.transpose(srow[:, t * P:(t + 1) * P],
                                            score[i][:, t:t + 1].to_broadcast([P, P]), ident[:, :])
                    last.then_inc(srow_ok, 1)
                it = item(half, j, 4, PAIRS)
                if it:
                    n, m, i = it
                    pe.wait_ge(exp_ok, n + 1)
                    if not first(n):
                        pe.wait_ge(OT_ok, n)
                    for b in range(2):
                        if b == 1 and not first(n):
                            pe.wait_ge(h1_ok, FIN * n)
                        for kt in range(R):
                            for qt in range(R):
                                last = pe.transpose(ET_ps[b][0:Q, kt * S + qt * Q:kt * S + (qt + 1) * Q],
                                                    E[i][:, R * b + qt, kt * Q:(kt + 1) * Q], ident[0:Q, 0:Q])
                        last.then_inc(ETp_ok, 1)
                it = item(half, j, 3, PAIRS)
                if it:
                    n, m, i = it
                    pe.wait_ge(qk_ok, n + 1)
                    pe.wait_ge(k0_ok, n + 1)
                    if not first(n):
                        pe.wait_ge(exp_ok, n)
                    for b in range(2):
                        for qt in range(R):
                            c0 = b * S + qt * Q
                            last = pe.matmul(S_ps[b][0:Q, qt * S:(qt + 1) * S], qk[i][:, c0:c0 + Q],
                                             k0[i][:, b * S:(b + 1) * S], start=True, stop=True)
                        last.then_inc(S_ok, 1)
                it = item(half, j, 2, PAIRS)
                if it:
                    n, m, i = it
                    pe.wait_ge(ranked, RANK * (n + 1))
                    pe.wait_ge(pre, PRE * (n + 1))
                    if not first(n):
                        pe.wait_ge(zT_ok, n)
                    for b in range(2):
                        for t in range(T):
                            g = T * b + t
                            last = pe.matmul(zT_ps[:, b * S:(b + 1) * S],
                                             zsplit[i][:, g, :, :].rearrange("p c d -> p (c d)"),
                                             onehot[i][:, g, :], start=(t == 0), stop=(t == T - 1))
                    last.then_inc(gathered, 1)
                it = item(half, j, 4, PAIRS)
                if it:
                    n, m, i = it
                    pe.wait_ge(v_ok, n + 1)
                    for b in range(2):
                        pe.wait_ge(ET_ok, 2 * n + b + 1)
                        for kt in range(R):
                            last = pe.matmul(OT_ps[b * D:(b + 1) * D, :], v[i][:, R * b + kt, 0:D],
                                             ET[b][:, kt * S:(kt + 1) * S], start=(kt == 0), stop=(kt == R - 1))
                    last.then_inc(OTp_ok, 1)
                it = item(half, j, 1, PAIRS)
                if it:
                    n, m, i = it
                    pe.wait_ge(cmp_ok, CMP * (n + 1))
                    if not first(n):
                        pe.wait_ge(zT_ok, n)
                    for b in range(2):
                        for t in range(T):
                            col = csum_ps[:, T * b + t:T * b + t + 1]
                            for a in range(t + 1):
                                c0 = a * T * P + (t - a) * P
                                last = pe.matmul(col, greater[:, b, c0:c0 + P], ones_bf[:, :],
                                                 start=(a == 0), stop=(a == t))
                    last.then_inc(csum_ok, 1)
                it = item(half, j, 2, PAIRS)
                if it:
                    n, m, i = it
                    pe.wait_ge(zT_ok, n + 1)
                    if not first(n):
                        pe.wait_ge(qk_ok, n)
                        pe.wait_ge(v_ok, n)
                    pe.matmul(qk_ps, wqk_hi[:, :], zT[i][:, :], start=True, stop=False)
                    pe.matmul(qk_ps, wqk_lo[:, :], zT[i][:, :], start=False, stop=True)
                    for g in range(G):
                        for w in (wvx_hi, wvx_lo):
                            last = pe.matmul(v_ps[:, g * VX:(g + 1) * VX], zT[i][:, g * Q:(g + 1) * Q], w[:, :],
                                             start=(w is wvx_hi), stop=(w is wvx_lo))
                    last.then_inc(qkv_ok, 1)
                it = item(half, j, 4, PAIRS)
                if it:
                    n, m, i = it
                    pe.wait_ge(OT_ok, n + 1)
                    pe.wait_ge(ET_ok, 2 * (n + 1))
                    for r in range(R):
                        last = pe.transpose(back_ps[:, r * P:(r + 1) * P], OT[:, r * Q:(r + 1) * Q], ident[:, :])
                    last.then_inc(back_ok, 1)

            run_a(pe, step_a)
            pe.wait_ge(h1_ok, FIN * PAIRS)
            pe.wait_ge(act_prep, ACT_PREP)
            pe.wait_ge(dve_prep, DVE_PREP)

            def step_b(half, j):
                prep, main, fin = (item(half, j, lag, UNITS) for lag in range(1, 4))
                for e in range(NE + 1):
                    if main and e < NE:
                        n, m, i = main
                        k = NE * n + e
                        if e == 0:
                            pe.wait_ge(mT_ok, n + 1)
                        if not first(n) or e:
                            pe.wait_ge(mb_ok, k)
                        pe.matmul(mb_ps[:, 0:C], spread[:, e, :], mT[i][:, :], start=True, stop=True)\
                            .then_inc(mbp_ok, 1)
                        if not first(n) or e >= 2:
                            pe.wait_ge(hid_ok, 2 * (k - 1))
                        for w in (w1_hi, w1_lo):
                            for c in range(2):
                                last = pe.matmul(hid_ps[e % 2][c][:, 0:C], w[:, e, :], uT[i][c][:, :],
                                                 start=(w is w1_hi), stop=(w is w1_lo))
                                if w is w1_lo:
                                    last.then_inc(hidp_ok, 1)
                    if main and e >= 1:
                        n, m, i = main
                        f = e - 1
                        k = NE * n + f
                        if not first(n) or f >= 2:
                            pe.wait_ge(ye_ok, k - 1)
                        for c in range(2):
                            pe.wait_ge(hid_ok, 2 * k + c + 1)
                            last = pe.matmul(y_ps[f % 2][c * D:(c + 1) * D, 0:C], w2_sb[:, f, :],
                                             hid[f % 2][c][:, :], start=True, stop=True)
                        last.then_inc(yp_ok, 1)
                    if prep and e < 2:
                        n, m, i = prep
                        if e == 0:
                            pe.wait_ge(ln, LN * (n + 1))
                            if not first(n):
                                pe.wait_ge(mT_ok, n)
                        else:
                            pe.wait_ge(uT_ok, 2 * n + 1)
                        for g in range(G):
                            last = pe.transpose(aux_ps[:, g * Q:(g + 1) * Q],
                                                usplit[:, G * e + g, :, :].rearrange("p c d -> p (c d)").bitcast(fp32),
                                                ident[0:Q, 0:Q])
                        last.then_inc(uTp_ok, 1)
                    if fin and e == 2:
                        n, m, i = fin
                        pe.wait_ge(acc_ok, (NE - 1) * (n + 1))
                        if prep:
                            pe.wait_ge(uT_ok, 2 * (prep[0] + 1))
                        for g in range(G):
                            last = pe.transpose(aux_ps[0:Q, g * P:(g + 1) * P], acc[i][:, g * Q:(g + 1) * Q],
                                                ident[:, :])
                        last.then_inc(backB_ok, 1)
                    if prep and e == 3:
                        n, m, i = prep
                        pe.wait_ge(uT_ok, 2 * (n + 1))
                        if fin:
                            pe.wait_ge(y_ok, fin[0] + 1)
                        for w in (wr_hi, wr_lo):
                            for c in range(2):
                                last = pe.matmul(aux_ps[0:2 * NE, 0:C], w[:, c, :], uT[i][c][:, :],
                                                 start=(w is wr_hi and c == 0), stop=(w is wr_lo and c == 1))
                        last.then_inc(lgTp_ok, 1)
                    if prep and e == 4:
                        n, m, i = prep
                        pe.wait_ge(lgT_ok, n + 1)
                        for g in range(G):
                            last = pe.matmul(aux_ps[0:Q, g * 2 * NE:(g + 1) * 2 * NE],
                                             lgT[:, g * Q:(g + 1) * Q], ident[0:2 * NE, 0:2 * NE],
                                             start=True, stop=True)
                        last.then_inc(lgp_ok, 1)
                    if prep and e == 7:
                        n, m, i = prep
                        pe.wait_ge(top, TOP * (n + 1))
                        for g in range(G):
                            last = pe.transpose(
                                aux_ps[0:4 * NE, g * Q:(g + 1) * Q],
                                msplit[:, g, :, :, :].rearrange("p a c e -> p (a c e)").bitcast(fp32),
                                ident[0:Q, 0:Q])
                        last.then_inc(mTp_ok, 1)

            run_b(pe, step_b)

        @block.vector
        def _(dve):
            dve.wait_ge(act_prep, 5)
            dve.tensor_tensor(wqk_lo[:, :], PS[0][:, 0:2 * D], wqk_hi[:, :], ALU.subtract).then_inc(dve_prep, 1)
            dve.tensor_tensor(wvx_lo[:, 0:D], PS[2][:, 0:D], wvx_hi[:, 0:D], ALU.subtract).then_inc(dve_prep, 1)
            dve.tensor_tensor(wvx_lo[:, D:VX], PS[0][:, 0:D + 1:D], wvx_hi[:, D:VX], ALU.subtract)\
                .then_inc(dve_prep, 1)
            dve.wait_ge(ffn_in, 16 * N_FFN)
            dve.wait_ge(w1_in, 16 * (N_W1 + 1))
            dve.tensor_scalar(w1_g[:, :, :], w1_raw[:, :, :], gamma_col[:, 0:1], None, ALU.mult)\
                .then_inc(dve_prep, 1)
            dve.tensor_scalar(wr_g[:, :], wr_raw[:, 0, :], gamma_col[:, 0:1], None, ALU.mult).then_inc(dve_prep, 1)
            dve.wait_ge(pe_prep, 3)
            dve.tensor_copy(b1_T[:, :], PS[3][:, NE:2 * NE]).then_inc(dve_prep, 1)
            dve.tensor_copy(b2_col[:, :], PS[3][:, 2 * NE:3 * NE]).then_inc(dve_prep, 1)
            dve.wait_ge(dve_prep, 6)
            dve.tensor_tensor(b1_eff[:, :], PS[3][:, 0:NE], b1_T[:, :], ALU.add).then_inc(dve_prep, 1)
            dve.tensor_tensor(br_eff[:, :], PS[3][0:2 * NE, 32:33], br_col[:, :], ALU.add).then_inc(dve_prep, 1)
            dve.wait_ge(act_prep, ACT_PREP)
            dve.tensor_tensor(w1_lo[:, :, :], w1_g[:, :, :], w1_hi[:, :, :], ALU.subtract).then_inc(dve_prep, 1)
            for c in range(2):
                cols = slice(NE * c, NE * (c + 1))
                dve.tensor_tensor(wr_lo[:, c, cols], wr_g[:, :], wr_hi[:, c, cols], ALU.subtract)\
                    .then_inc(dve_prep, 1)
            dve.wait_ge(cst_in, 16 * N_CST)

            def pre_score(it):
                n, m, i = it
                if isinstance(n, int) and n < 3:
                    dve.wait_ge(x_in[n], 16)
                Xn = X[:, bass.ds(TT * n, TT), :]
                dve.tensor_tensor(xw[:, :].rearrange("p (t d) -> p t d", d=D), Xn,
                                  w_bc[:, None, :].to_broadcast([P, TT, D]), ALU.mult).then_inc(pre, 1)
                dve.wait_ge(pre, PRE * n + 1)
                dve.tensor_reduce(ssum[:, :], xw[:, :].rearrange("p (t d) -> p t d", d=D), AX.X, ALU.add)\
                    .then_inc(pre, 1)
                dve.wait_ge(pre, PRE * n + 2)
                dve.tensor_scalar(score[i][:, :], ssum[:, :], b_col[:, 0:1], None, ALU.add).then_inc(pre, 1)

            def pre_gate(it):
                n, m, i = it
                Xn = X[:, bass.ds(TT * n, TT), :]
                dve.wait_ge(expneg_ok, n + 1)
                dve.tensor_scalar(gate1[:, :], expneg[:, :], 1.0, None, ALU.add).then_inc(pre, 1)
                dve.wait_ge(pre, PRE * n + 4)
                dve.reciprocal(gate[:, :], gate1[:, :]).then_inc(pre, 1)
                dve.wait_ge(pre, PRE * n + 5)
                if not first(n, 2):
                    dve.wait_ge(hb_ok, n - 1)
                dve.tensor_tensor(h[i][:, :, :], Xn, gate[:, :, None].to_broadcast([P, TT, D]), ALU.mult)\
                    .then_inc(pre, 1)
                dve.wait_ge(pre, PRE * n + 6)
                dve.tensor_reduce(hsum[:, :], h[i][:, :, :], AX.X, ALU.add).then_inc(pre, 1)
                dve.wait_ge(pre, PRE * n + 7)
                dve.tensor_scalar(hmean[:, :], hsum[:, :], 1.0 / D, None, ALU.mult).then_inc(pre, 1)
                dve.wait_ge(pre, PRE * n + 8)
                dve.tensor_tensor(hc[:, :, :], h[i][:, :, :], hmean[:, :, None].to_broadcast([P, TT, D]),
                                  ALU.subtract).then_inc(pre, 1)

            def pre_var(it):
                n, m, i = it
                dve.wait_ge(sq_ok, n + 1)
                dve.tensor_reduce(sqsum[:, :], sq[:, :, :], AX.X, ALU.add).then_inc(pre, 1)
                dve.wait_ge(pre, PRE * n + 10)
                dve.tensor_scalar(hvar[:, :], sqsum[:, :], 1.0 / D, EPS, ALU.mult, ALU.add).then_inc(pre, 1)

            def pre_z(it):
                n, m, i = it
                dve.wait_ge(rstd_ok, n + 1)
                dve.tensor_tensor(z[:, :, :], hc[:, :, :], rstd[:, :, None].to_broadcast([P, TT, D]), ALU.mult)\
                    .then_inc(pre, 1)
                dve.wait_ge(zhi_ok, n + 1)
                dve.tensor_tensor(zsplit[i][:, :, 1, :], z[:, :, :], zsplit[i][:, :, 0, :], ALU.subtract)\
                    .then_inc(pre, 1)

            def compare(it):
                n, m, i = it
                dve.wait_ge(srow_ok, n + 1)
                if not first(n):
                    dve.wait_ge(csum_ok, n)
                    dve.wait_ge(ranked, RANK * n)
                for b in range(2):
                    for t in range(T):
                        c0, w = t * T * P, (T - t) * P
                        g = T * b + t
                        dve.scalar_tensor_tensor(
                            out=greater[:, b, c0:c0 + w], in0=srow[:, (g * P):(T * b + T) * P],
                            scalar=score[i][:, g:g + 1], in1=later[:, 0:w], op0=ALU.is_gt, op1=ALU.mult,
                            accum_out=rowsum[:, g:g + 1]).then_inc(cmp_ok, 1)

            def make_onehot(it):
                n, m, i = it
                dve.wait_ge(csum_ok, n + 1)
                dve.wait_ge(cmp_ok, CMP * (n + 1))
                dve.tensor_tensor(ahead[:, :], rowsum[:, :], csum_ps, ALU.subtract).then_inc(ranked, 1)
                dve.wait_ge(ranked, RANK * n + 1)
                if not first(n, 2):
                    dve.wait_ge(scattered[i], 16 * TT * m)
                    dve.wait_ge(gathered, n - 1)
                dve.tensor_tensor(row_of[i][:, :], ahead[:, :], row_index[:, bass.ds(TT * n, TT)], ALU.add)\
                    .then_inc(ranked, 1)
                dve.tensor_tensor(rank[:, :], ahead[:, :], index[:, :], ALU.add).then_inc(ranked, 1)
                dve.wait_ge(ranked, RANK * n + 3)
                for g in range(TT):
                    dve.tensor_scalar(onehot[i][:, g, :], position[:, :], rank[:, g:g + 1], None, ALU.is_equal)\
                        .then_inc(ranked, 1)

            def row_max(it):
                n, m, i = it
                for b in range(2):
                    dve.wait_ge(S_ok, 2 * n + b + 1)
                    dve.tensor_reduce(smax[:, R * b:R * (b + 1)],
                                      S_ps[b][0:Q, 0:R * S].rearrange("p (r s) -> p r s", r=R), AX.X, ALU.max)\
                        .then_inc(max_ok, 1)
                dve.wait_ge(max_ok, MAX * n + 2)
                if not first(n, 2):
                    dve.wait_ge(exp_ok, n - 1)
                dve.tensor_scalar(nmax[i][:, :], smax[:, :], -SCALE, None, ALU.mult).then_inc(max_ok, 1)

            def kv_out(it):
                n, m, i = it
                dve.wait_ge(qkv_ok, n + 1)
                if not first(n, 2):
                    dve.wait_ge(OTp_ok, n - 1)
                dve.tensor_tensor(v[i][:, :, :], v_ps.rearrange("p (g c) -> p g c", g=G),
                                  vbias[:, None, :].to_broadcast([Q, G, VX]), ALU.add).then_inc(v_ok, 1)
                dve.wait_ge(qk_ok, n + 1)
                if not first(n, 2):
                    dve.wait_ge(S_ok, 2 * (n - 1))
                dve.tensor_copy(k0[i][0:D, :], qk[i][D:P, :]).then_inc(k0_ok, 1)

            def residual(it):
                n, m, i = it
                dve.wait_ge(exp_ok, n + 1)
                dve.wait_ge(v_ok, n + 1)
                dve.reciprocal(rden[:, :], den[i][:, :]).then_inc(h1_ok, 1)
                dve.wait_ge(h1_ok, FIN * n + 1)
                dve.scalar_tensor_tensor(out=rden_q[:, :], in0=v[i][:, :, D], scalar=0.0, in1=rden[:, :],
                                         op0=ALU.not_equal, op1=ALU.mult).then_inc(h1_ok, 1)
                dve.wait_ge(h1_ok, FIN * n + 2)
                dve.scalar_tensor_tensor(out=rden_qk[:, :], in0=v[i][:, :, D + 1], scalar=0.0, in1=rden_q[:, :],
                                         op0=ALU.not_equal, op1=ALU.mult).then_inc(h1_ok, 1)
                dve.wait_ge(h1_ok, FIN * n + 3)
                dve.wait_ge(back_ok, n + 1)
                for b in range(2):
                    last = dve.tensor_tensor(
                        attn[:, b, :, :], back_ps.rearrange("p (r b d) -> p b r d", r=R, b=2)[:, b, :, :],
                        rden_qk[:, R * b:R * (b + 1), None].to_broadcast([Q, R, D]), ALU.mult)
                last.then_inc(h1_ok, 1)
                dve.wait_ge(h1_ok, FIN * n + 4)
                dve.wait_ge(h0_in[i], 16 * (m + 1))
                H1n = H1[:, bass.ds(n, 1), :].rearrange("p a f -> p (a f)")
                dve.tensor_tensor(H1n, attn[:, :, :, :].rearrange("p b r d -> p (b r d)"), H1n, ALU.add)\
                    .then_inc(h1_ok, 1)

            def step_a(half, j):
                if isinstance(half, int) and half == 1 and j == 1:
                    dve.wait_ge(x_in[3], 16)
                order = [(compare, 1), (pre_score, 0), (row_max, 3), (pre_gate, 0), (make_onehot, 1),
                         (pre_var, 0), (kv_out, 2), (residual, 4), (pre_z, 0)]
                for stage, lag in order:
                    it = item(half, j, lag, PAIRS)
                    if it:
                        stage(it)

            dve.wait_ge(pool_prep, POOL_PREP)
            run_a(dve, step_a)

            def norm(it, part):
                n, m, i = it
                rows = H1[:, bass.ds(2 * n, 2), :].rearrange("p c (g d) -> p (c g) d", d=D)
                if part == 0:
                    dve.tensor_reduce(usum[:, :], rows, AX.X, ALU.add).then_inc(ln, 1)
                    dve.wait_ge(ln, LN * n + 1)
                    dve.tensor_scalar(umean[:, :], usum[:, :], 1.0 / D, None, ALU.mult).then_inc(ln, 1)
                    dve.wait_ge(ln, LN * n + 2)
                    dve.tensor_tensor(uc[:, :, :], rows, umean[:, :, None].to_broadcast([Q, TU, D]), ALU.subtract)\
                        .then_inc(ln, 1)
                if part == 1:
                    dve.wait_ge(usq_ok, n + 1)
                    dve.tensor_reduce(usqsum[:, :], usq[:, :, :], AX.X, ALU.add).then_inc(ln, 1)
                    dve.wait_ge(ln, LN * n + 4)
                    dve.tensor_scalar(uvar[:, :], usqsum[:, :], (1.0 + EPS) / D, EPS * EPS, ALU.mult, ALU.add)\
                        .then_inc(ln, 1)
                if part == 2:
                    dve.wait_ge(urstd_ok, n + 1)
                    dve.tensor_tensor(uz[:, :, :], uc[:, :, :], urstd[:, :, None].to_broadcast([Q, TU, D]),
                                      ALU.mult).then_inc(ln, 1)
                    dve.wait_ge(uhi_ok, n + 1)
                    dve.tensor_tensor(usplit[:, :, 1, :], uz[:, :, :], usplit[:, :, 0, :], ALU.subtract)\
                        .then_inc(ln, 1)

            def first_top(k0_, n, src, top_, is_, pr_, pm_, sel_):
                def bc(a):
                    return a[:, :, None].to_broadcast([Q, TU, NE])
                dve.tensor_reduce(top_[:, :], src[:, :, :], AX.X, ALU.max).then_inc(top, 1)
                dve.wait_ge(top, TOP * n + k0_ + 1)
                dve.tensor_tensor(is_[:, :, :], src[:, :, :], bc(top_), ALU.is_equal).then_inc(top, 1)
                dve.wait_ge(top, TOP * n + k0_ + 2)
                dve.tensor_tensor(pr_[:, :, :], is_[:, :, :], falling[:, None, :].to_broadcast([Q, TU, NE]),
                                  ALU.mult).then_inc(top, 1)
                dve.wait_ge(top, TOP * n + k0_ + 3)
                dve.tensor_reduce(pm_[:, :], pr_[:, :, :], AX.X, ALU.max).then_inc(top, 1)
                dve.wait_ge(top, TOP * n + k0_ + 4)
                dve.tensor_tensor(sel_[:, :, :], pr_[:, :, :], bc(pm_), ALU.is_equal).then_inc(top, 1)
                dve.wait_ge(top, TOP * n + k0_ + 5)

            def route(it, part):
                n, m, i = it

                def bc(a):
                    return a[:, :, None].to_broadcast([Q, TU, NE])

                def flat(a):
                    return a[:, :, :].rearrange("p g e -> p (g e)")
                if part == 0:
                    dve.wait_ge(lgp_ok, n + 1)
                    for c in range(2):
                        last = dve.tensor_copy(
                            lg[:, G * c:G * (c + 1), :],
                            aux_ps[0:Q, 0:TU * NE].rearrange("p (g c e) -> p c g e", g=G, c=2)[:, c, :, :])
                    last.then_inc(top, 1)
                    dve.wait_ge(top, TOP * n + 1)
                    first_top(1, n, lg, top1, is1, pr1, pm1, sel1)
                    dve.scalar_tensor_tensor(out=flat(lg2), in0=flat(sel1), scalar=-3e38, in1=flat(lg),
                                             op0=ALU.mult, op1=ALU.add).then_inc(top, 1)
                    dve.wait_ge(top, TOP * n + 7)
                    dve.tensor_reduce(top2[:, :], lg2[:, :, :], AX.X, ALU.max).then_inc(top, 1)
                    dve.wait_ge(top, TOP * n + 8)
                    dve.tensor_tensor(is2[:, :, :], lg2[:, :, :], bc(top2), ALU.is_equal).then_inc(top, 1)
                    dve.wait_ge(top, TOP * n + 9)
                    dve.tensor_tensor(pr2[:, :, :], is2[:, :, :], falling[:, None, :].to_broadcast([Q, TU, NE]),
                                      ALU.mult).then_inc(top, 1)
                    dve.wait_ge(top, TOP * n + 10)
                    dve.tensor_reduce(pm2[:, :], pr2[:, :, :], AX.X, ALU.max).then_inc(top, 1)
                    dve.tensor_tensor(gap[:, :], top1[:, :], top2[:, :], ALU.subtract).then_inc(top, 1)
                    dve.wait_ge(top, TOP * n + 12)
                    dve.tensor_tensor(sel2[:, :, :], pr2[:, :, :], bc(pm2), ALU.is_equal).then_inc(top, 1)
                if part == 1:
                    dve.wait_ge(tanh_ok, n + 1)
                    dve.tensor_scalar(wt1[:, :], tanh[:, :], 0.5, 0.5, ALU.mult, ALU.add).then_inc(top, 1)
                    dve.tensor_scalar(wt2[:, :], tanh[:, :], -0.5, 0.5, ALU.mult, ALU.add).then_inc(top, 1)
                    dve.wait_ge(top, TOP * n + 15)
                    dve.tensor_tensor(mix1[:, :, :], sel1[:, :, :], bc(wt1), ALU.mult).then_inc(top, 1)
                    dve.tensor_tensor(mix2[:, :, :], sel2[:, :, :], bc(wt2), ALU.mult).then_inc(top, 1)
                    dve.wait_ge(top, TOP * n + 17)
                    dve.tensor_tensor(mix[:, :, :], mix1[:, :, :], mix2[:, :, :], ALU.add).then_inc(top, 1)
                    dve.wait_ge(top, TOP * n + 18)
                    if not first(n):
                        dve.wait_ge(mTp_ok, n)
                    for c in range(2):
                        last = dve.tensor_copy(msplit[:, :, 0, c, :], mix[:, G * c:G * (c + 1), :])
                    last.then_inc(top, 1)
                    dve.wait_ge(top, TOP * n + 19)
                    for c in range(2):
                        last = dve.tensor_tensor(msplit[:, :, 1, c, :], mix[:, G * c:G * (c + 1), :],
                                                 msplit[:, :, 0, c, :], ALU.subtract)
                    last.then_inc(top, 1)

            def step_b(half, j):
                nxt, prep, main, fin = (item(half, j, lag, UNITS) for lag in range(4))
                for e in range(NE):
                    if main:
                        n, m, i = main
                        k = NE * n + e
                        dve.wait_ge(yp_ok, k + 1)
                        dve.wait_ge(mb_ok, k + 1)
                        if e == 0:
                            if not first(n, 2):
                                dve.wait_ge(backB_ok, n - 1)
                        elif not first(n) or e > 2:
                            dve.wait_ge(acc_ok, (NE - 1) * n + max(e - 2, 0))
                        dst = ye[e % 2] if e else acc[i]
                        dve.scalar_tensor_tensor(out=dst[:, :], in0=y_ps[e % 2][:, 0:C], scalar=b2_col[:, e:e + 1],
                                                 in1=mb[e % 2][:, :], op0=ALU.add, op1=ALU.mult).then_inc(ye_ok, 1)
                    if prep and e == 4:
                        route(prep, 0)
                    if prep and e == 5:
                        route(prep, 1)
                    if nxt and e == 6:
                        norm(nxt, 0)
                        norm(nxt, 1)
                        norm(nxt, 2)
                    if fin and e == 1:
                        n, m, i = fin
                        dve.wait_ge(backB_ok, n + 1)
                        for c in range(2):
                            last = dve.tensor_tensor(
                                y[:, bass.ds(2 * n + c, 1), :, :].rearrange("p a g d -> p (a g) d"), aux_ps[0:Q, :].rearrange("p (g c d) -> p c g d", g=G, c=2)[:, c],
                                H1[:, bass.ds(2 * n + c, 1), :].rearrange("p a (g d) -> p (a g) d", d=D), ALU.add)
                        last.then_inc(y_ok, 1)

            run_b(dve, step_b)


POOL_PREP = 10 + 4 + 3 + 2
ACT_PREP = 9
DVE_PREP_PSUM = 9
DVE_PREP = 12

_INS = ['x', 'L0_tok_w', 'L0_tok_b', 'L0_attn_Wq', 'L0_attn_bq', 'L0_attn_Wk', 'L0_attn_bk', 'L0_attn_Wv',
        'L0_attn_bv', 'L0_attn_Wo', 'L0_attn_bo', 'L0_ffn_gamma', 'L0_ffn_beta', 'L0_ffn_Wr', 'L0_ffn_br',
        'L0_ffn_W1', 'L0_ffn_b1', 'L0_ffn_W2', 'L0_ffn_b2']
KEPT = 0.8


def kernel(**inputs):
    import numpy as _np
    import concourse.bacc as _bacc
    from concourse import mybir as _mybir
    from concourse.bass_utils import run_bass_kernel_spmd as _run

    nc = _bacc.Bacc("TRN2", target_bir_lowering=False, num_devices=1)
    arrays, args = {}, []
    for name in _INS:
        a = _np.ascontiguousarray(inputs[name])
        arrays[f"in_{name}"] = a
        args.append(nc.dram_tensor(f"in_{name}", a.shape, _mybir.dt.from_np(a.dtype), kind="ExternalInput").ap())
    b, n, d = inputs['x'].shape
    args.append(nc.dram_tensor("out_0", (b, max(1, int(n * KEPT)), d), _mybir.dt.float32, kind="ExternalOutput").ap())
    audio_tower_kernel(nc, *args)
    r = _run(nc, [arrays], core_ids=[0])
    return r.results[0]["out_0"]
```

```python
import concourse.bass as bass
from concourse import mybir
from concourse.alu_op_type import AluOpType as ALU
from contextlib import ExitStack


def audio_tower_kernel(
    nc: bass.Bass,
    x: bass.AP,
    tok_w: bass.AP,
    tok_b: bass.AP,
    Wq: bass.AP,
    bq: bass.AP,
    Wk: bass.AP,
    bk: bass.AP,
    Wv: bass.AP,
    bv: bass.AP,
    Wo: bass.AP,
    bo: bass.AP,
    gamma: bass.AP,
    beta: bass.AP,
    Wr: bass.AP,
    br: bass.AP,
    W1: bass.AP,
    b1: bass.AP,
    W2: bass.AP,
    b2: bass.AP,
    out: bass.AP,
):
    fp32 = mybir.dt.float32
    fp32r = mybir.dt.float32r
    bf16 = mybir.dt.bfloat16
    i32 = mybir.dt.int32
    ACT = mybir.ActivationFunctionType
    AX = mybir.AxisListType

    B, N, D = x.shape
    S = out.shape[1]
    P = 128
    T = N // P
    R = 2
    Q = S // R
    NE, HID = W1.shape[0], W1.shape[2]
    PAIRS = B // 2
    UNITS = PAIRS // 2
    TT = 2 * T
    G = 2 * R
    TU = 2 * G
    C = 2 * S
    VX = D + 2
    SCALE = float(D) ** -0.5
    EPS = 1e-5

    x_tiles = x.rearrange("b (t p) d -> p (b t) d", p=P)
    h_sorted = nc.dram_tensor("h_sorted", (B * N, D), fp32).ap()
    h_rows = h_sorted.rearrange("(b n) d -> b n d", b=B)[:, 0:S, :].rearrange("b (p r) d -> p b (r d)", r=R)
    out_rows = out.rearrange("b (p r) d -> p b (r d)", r=R)

    ctx = ExitStack()
    with ctx:
        def sb(name, shape, dt=fp32):
            return ctx.enter_context(nc.sbuf_tensor(name, shape, dt))

        def sem(name):
            return ctx.enter_context(nc.semaphore(name))

        ident = sb("ident", [P, P])
        later = sb("later", [P, T * P])
        ones_bf = sb("ones_bf", [P, 1], bf16)
        row_index = sb("row_index", [P, B * T])
        neg_half = sb("neg_half", [Q, TU])
        falling = sb("falling", [Q, NE])
        w_bc = sb("w_bc", [P, D])
        b_col = sb("b_col", [P, 1])
        bo_bc = sb("bo_bc", [P, D])
        wqk_nat = sb("wqk_nat", [D, 4, D])
        wv_nat = sb("wv_nat", [D, 2, D])
        wo_nat = sb("wo_nat", [D, D])
        woT = sb("woT", [D, D])
        bqk_col = sb("bqk_col", [P, 1])
        bv_col = sb("bv_col", [D, 1])
        wqk_hi = sb("wqk_hi", [P, 2 * D], fp32r)
        wqk_lo = sb("wqk_lo", [P, 2 * D], fp32r)
        wvx_hi = sb("wvx_hi", [P, VX], fp32r)
        wvx_lo = sb("wvx_lo", [P, VX], fp32r)
        vbias = sb("vbias", [Q, VX])
        gamma_col = sb("gamma_col", [P, 1])
        beta_col = sb("beta_col", [D, 1])
        wr_raw = sb("wr_raw", [P, NE])
        wr_g = sb("wr_g", [P, NE])
        wr_split = sb("wr_split", [P, 2, NE], fp32r)
        br_bc = sb("br_bc", [Q, NE])
        br_eff = sb("br_eff", [Q, NE])
        w1_raw = sb("w1_raw", [P, NE, HID])
        w1_g = sb("w1_g", [P, NE, HID])
        w1_hi = sb("w1_hi", [P, NE, HID], fp32r)
        w1_lo = sb("w1_lo", [P, NE, HID], fp32r)
        b1_nat = sb("b1_nat", [NE, HID])
        b1_T = sb("b1_T", [HID, NE])
        b1_eff = sb("b1_eff", [HID, NE])
        w2_sb = sb("w2_sb", [HID, NE, D])
        b2_nat = sb("b2_nat", [NE, 2 * D])
        b2_col = sb("b2_col", [P, NE])
        pick = sb("pick", [P, NE, 2, D])
        spread = sb("spread", [P, NE, P], fp32r)

        X = sb("X", [P, B * T, D])
        H1 = sb("H1", [Q, PAIRS, G * D])
        xw = sb("xw", [P, TT * D])
        ssum = sb("ssum", [P, TT])
        score = [sb(f"score{i}", [P, TT]) for i in range(2)]
        expneg = sb("expneg", [P, TT])
        gate1 = sb("gate1", [P, TT])
        gate = sb("gate", [P, TT])
        h = [sb(f"h{i}", [P, TT, D]) for i in range(2)]
        greater = sb("greater", [P, 2, (T + 1) * P], bf16)
        rowsum = sb("rowsum", [P, TT])
        ahead = sb("ahead", [P, TT])
        row_of = [sb(f"row_of{i}", [P, TT], i32) for i in range(2)]
        H0 = [sb(f"H0_{i}", [Q, G, D]) for i in range(2)]
        hsum = sb("hsum", [Q, G])
        hc = sb("hc", [Q, G, D])
        sq = sb("sq", [Q, G, D])
        hvar = sb("hvar", [Q, G])
        hvar_eps = sb("hvar_eps", [Q, G])
        rstd = sb("rstd", [Q, G])
        z = sb("z", [Q, G, D])
        zsplit = [sb(f"zsplit{i}", [Q, G, 2, D], fp32r) for i in range(2)]
        zT = [sb(f"zT{i}", [P, C], fp32r) for i in range(2)]
        qk = [sb(f"qk{i}", [P, C]) for i in range(2)]
        k0 = [sb(f"k0_{i}", [P, C]) for i in range(2)]
        v = [sb(f"v{i}", [Q, G, VX]) for i in range(2)]
        smax = sb("smax", [Q, G])
        nmax = [sb(f"nmax{i}", [Q, G]) for i in range(2)]
        E = [sb(f"E{i}", [Q, G, S]) for i in range(2)]
        den = [sb(f"den{i}", [Q, G]) for i in range(2)]
        ET = [sb(f"ET{i}", [Q, R * S]) for i in range(2)]
        OT = sb("OT", [P, S])
        rden = sb("rden", [Q, G])
        rden_q = sb("rden_q", [Q, G])
        rden_qk = [sb(f"rden_qk{i}", [Q, G]) for i in range(2)]
        attn = sb("attn", [Q, 2, R, D])

        usum = sb("usum", [Q, TU])
        uc = sb("uc", [Q, TU, D])
        usq = sb("usq", [Q, TU, D])
        uvar = sb("uvar", [Q, TU])
        uvar_eps = sb("uvar_eps", [Q, TU])
        urstd = sb("urstd", [Q, TU])
        uz = sb("uz", [Q, TU, D])
        usplit = sb("usplit", [Q, TU, 2, D], fp32r)
        uT = [[sb(f"uT{i}_{c}", [P, C], fp32r) for c in range(2)] for i in range(2)]
        lg_hi = sb("lg_hi", [Q, TU, NE])
        lg = sb("lg", [Q, TU, NE])
        top1 = sb("top1", [Q, TU])
        is1 = sb("is1", [Q, TU, NE])
        pr1 = sb("pr1", [Q, TU, NE])
        pm1 = sb("pm1", [Q, TU])
        sel1 = sb("sel1", [Q, TU, NE])
        lg2 = sb("lg2", [Q, TU, NE])
        top2 = sb("top2", [Q, TU])
        is2 = sb("is2", [Q, TU, NE])
        pr2 = sb("pr2", [Q, TU, NE])
        pm2 = sb("pm2", [Q, TU])
        sel2 = sb("sel2", [Q, TU, NE])
        gap = sb("gap", [Q, TU])
        tanh = sb("tanh", [Q, TU])
        wt1 = sb("wt1", [Q, TU])
        wt2 = sb("wt2", [Q, TU])
        mix1 = sb("mix1", [Q, TU, NE])
        mix2 = sb("mix2", [Q, TU, NE])
        mix = sb("mix", [Q, TU, NE])
        msplit = sb("msplit", [Q, G, 2, 2, NE], fp32r)
        mT = [sb(f"mT{i}", [P, C], fp32r) for i in range(2)]
        hid = [[sb(f"hid{i}_{c}", [HID, C]) for c in range(2)] for i in range(2)]
        mb = [sb(f"mb{i}", [P, C]) for i in range(2)]
        ye = [sb(f"ye{i}", [P, C]) for i in range(2)]
        acc = [sb(f"acc{i}", [P, C]) for i in range(2)]
        y = sb("y", [Q, PAIRS, G, D])

        PS = [ctx.enter_context(nc.psum_tensor(f"PS{i}", [P, 512], fp32)) for i in range(8)]
        srow = PS[0]
        zT_ps = PS[1][:, 0:C]
        qk_ps = PS[2][:, 0:C]
        v_ps, csum_ps = PS[3][0:Q, 0:G * VX], PS[3][:, G * VX:G * VX + TT]
        S_ps = [PS[4], PS[5]]
        ET_ps = [PS[6], PS[7]]
        OT_ps = PS[6][:, 0:S]
        back_ps = PS[7][0:Q, 0:R * P]
        hid_ps = [[PS[0], PS[1]], [PS[2], PS[3]]]
        y_ps = [PS[4], PS[5]]
        mb_ps = PS[6]
        aux_ps = PS[7]

        x_in = [sem(f"x_in{i}") for i in range(4)]
        cst_in, attn_in, ffn_in, w1_in = sem("cst_in"), sem("attn_in"), sem("ffn_in"), sem("w1_in")
        N_CST, N_ATTN, N_FFN, N_W1 = 3, 12, 9, 2
        pool_prep, pool_cst, pe_prep, act_prep, dve_prep = (
            sem("pool_prep"), sem("pool_cst"), sem("pe_prep"), sem("act_prep"), sem("dve_prep"))
        PRE = 6
        pre = sem("pre")
        expneg_ok, srow_ok, csum_ok = sem("expneg_ok"), sem("srow_ok"), sem("csum_ok")
        CMP, RANK = TT, 2
        cmp_ok, ranked = sem("cmp_ok"), sem("ranked")
        scattered = [sem(f"scattered{i}") for i in range(2)]
        h0_in = [sem(f"h0_in{i}") for i in range(2)]
        NRM = 4
        nrm = sem("nrm")
        hb_ok, sq_ok, rstd_ok, z_ok, zhi_ok, zlo_ok = (
            sem("hb_ok"), sem("sq_ok"), sem("rstd_ok"), sem("z_ok"), sem("zhi_ok"), sem("zlo_ok"))
        zTp_ok, zT_ok = sem("zTp_ok"), sem("zT_ok")
        qkv_ok, qk_ok, k0_ok, v_ok = sem("qkv_ok"), sem("qk_ok"), sem("k0_ok"), sem("v_ok")
        S_ok, max_ok, exp_ok = sem("S_ok"), sem("max_ok"), sem("exp_ok")
        MAX, SCL, FIN = 3, 3, 2
        scaled = sem("scaled")
        ETp_ok, ET_ok, OTp_ok, OT_ok, back_ok = (
            sem("ETp_ok"), sem("ET_ok"), sem("OTp_ok"), sem("OT_ok"), sem("back_ok"))
        h1_ok = sem("h1_ok")
        LN = 5
        ln, usq_ok, urstd_ok, uhi_ok, ulo_ok = (
            sem("ln"), sem("usq_ok"), sem("urstd_ok"), sem("uhi_ok"), sem("ulo_ok"))
        uTp_ok, uT_ok = sem("uTp_ok"), sem("uT_ok")
        lgp_ok = sem("lgp_ok")
        TOP = 23
        top, tanh_ok = sem("top"), sem("tanh_ok")
        mTp_ok, mT_ok = sem("mTp_ok"), sem("mT_ok")
        mbp_ok, mb_ok = sem("mbp_ok"), sem("mb_ok")
        hidp_ok, hid_ok, yp_ok, ye_ok, acc_ok = (
            sem("hidp_ok"), sem("hid_ok"), sem("yp_ok"), sem("ye_ok"), sem("acc_ok"))
        backB_ok, y_ok = sem("backB_ok"), sem("y_ok")
        stored = sem("stored")

        block = ctx.enter_context(nc.Block())

        def item(half, j, lag, count):
            m = half + (j - lag) // 2
            n = 2 * half + (j - lag)
            if isinstance(half, int) and not 0 <= n < count:
                return None
            return n, m, (j - lag) % 2

        A_LAG, B_LAG = 8, 3

        def run_a(eng, step):
            for s in range(A_LAG):
                step(s // 2, s % 2)
            with eng.Fori(A_LAG // 2, PAIRS // 2) as half:
                step(half, 0)
                step(half, 1)
            for s in range(PAIRS, PAIRS + A_LAG):
                step(s // 2, s % 2)

        def run_b(eng, step):
            for s in range(B_LAG + 1):
                step(s // 2, s % 2)
            with eng.Fori((B_LAG + 1) // 2, UNITS // 2) as half:
                step(half, 0)
                step(half, 1)
            for s in range(UNITS, UNITS + B_LAG):
                step(s // 2, s % 2)

        def first(n, k=1):
            return isinstance(n, int) and n < k

        @block.sync
        def _(sp):
            cuts = [0, 1, 2, 4, PAIRS]
            sp.dma_start(X[:, 0:TT, :], x_tiles[:, 0:TT, :]).then_inc(x_in[0], 16)
            sp.dma_start(w_bc[:, :], tok_w.partition_broadcast(P)).then_inc(cst_in, 16)
            sp.dma_start(b_col[:, :], tok_b.partition_broadcast(P)).then_inc(cst_in, 16)
            sp.dma_start(bo_bc[:, :], bo.partition_broadcast(P)).then_inc(cst_in, 16)
            for i in (1, 2):
                a, b = TT * cuts[i], TT * cuts[i + 1]
                sp.dma_start(X[:, a:b, :], x_tiles[:, a:b, :]).then_inc(x_in[i], 16)
            for i in range(2):
                sp.dma_start(wqk_nat[:, i, :], Wq).then_inc(attn_in, 16)
                sp.dma_start(wqk_nat[:, 2 + i, :], Wk).then_inc(attn_in, 16)
                sp.dma_start(wv_nat[:, i, :], Wv).then_inc(attn_in, 16)
            sp.dma_start(wo_nat[:, :], Wo).then_inc(attn_in, 16)
            sp.dma_start(bqk_col[0:D, :], bq.unsqueeze(1)).then_inc(attn_in, 16)
            sp.dma_start(bqk_col[D:P, :], bk.unsqueeze(1)).then_inc(attn_in, 16)
            sp.dma_start(bv_col[:, :], bv.unsqueeze(1)).then_inc(attn_in, 16)
            sp.dma_start(vbias[:, D:D + 1], bq[0:1].partition_broadcast(Q)).then_inc(attn_in, 16)
            sp.dma_start(vbias[:, D + 1:VX], bk[0:1].partition_broadcast(Q)).then_inc(attn_in, 16)
            a, b = TT * cuts[3], TT * cuts[4]
            sp.dma_start(X[:, a:b, :], x_tiles[:, a:b, :]).then_inc(x_in[3], 16)
            for i in range(2):
                rows = slice(i * D, (i + 1) * D)
                sp.dma_start(gamma_col[rows, :], gamma.unsqueeze(1)).then_inc(ffn_in, 16)
                sp.dma_start(wr_raw[rows, :], Wr).then_inc(ffn_in, 16)
                sp.dma_start(b2_nat[:, i * D:(i + 1) * D], b2).then_inc(ffn_in, 16)
                sp.dma_start(w1_raw[rows, :, :], W1.rearrange("e d h -> d e h")).then_inc(w1_in, 16)
            sp.dma_start(br_bc[:, :], br.partition_broadcast(Q)).then_inc(ffn_in, 16)
            sp.dma_start(beta_col[:, :], beta.unsqueeze(1)).then_inc(ffn_in, 16)
            sp.dma_start(b1_nat[:, :], b1).then_inc(ffn_in, 16)
            sp.dma_start(w2_sb[:, :, :], W2.rearrange("e h d -> h e d")).then_inc(w1_in, 16)

            def step_a(half, j):
                it = item(half, j, 2, PAIRS)
                if it:
                    n, m, i = it
                    sp.wait_ge(scattered[i], 16 * TT * (m + 1))
                    sp.dma_start(H0[i][:, :, :].rearrange("p (b r) d -> p b (r d)", b=2),
                                 h_rows[:, bass.ds(2 * n, 2), :]).then_inc(h0_in[i], 16)

            run_a(sp, step_a)

            def step_b(half, j):
                it = item(half, j, 3, UNITS)
                if it:
                    n, m, i = it
                    sp.wait_ge(y_ok, n + 1)
                    sp.dma_start(out_rows[:, bass.ds(4 * n, 4), :],
                                 y[:, bass.ds(2 * n, 2), :, :].rearrange("p c (b r) d -> p (c b) (r d)", r=R))\
                        .then_inc(stored, 16)

            run_b(sp, step_b)
            sp.wait_ge(stored, 16 * UNITS)

        @block.gpsimd
        def _(pool):
            pool.memset(ident[:, :], 0.0).then_inc(pool_prep, 1)
            pool.memset(later[:, :], 1.0).then_inc(pool_prep, 1)
            pool.memset(ones_bf[:, :], 1.0).then_inc(pool_prep, 1)
            pool.memset(neg_half[:, :], -0.5).then_inc(pool_prep, 1)
            pool.wait_ge(pool_prep, 4)
            pool.affine_select(out=ident[:, :], in_=ident[:, :], compare_op=ALU.not_equal, fill=1.0,
                               base=0, pattern=[[-1, P]], channel_multiplier=1).then_inc(pool_prep, 1)
            pool.affine_select(out=later[:, :], in_=later[:, :], compare_op=ALU.is_gt, fill=0.0,
                               base=0, pattern=[[1, T * P]], channel_multiplier=-1).then_inc(pool_prep, 1)
            pool.iota(row_index[:, :], pattern=[[N, B], [P, T]], base=0, channel_multiplier=1,
                      allow_small_or_imprecise_dtypes=True).then_inc(pool_prep, 1)
            pool.iota(falling[:, :], pattern=[[-1, NE]], base=NE, channel_multiplier=0,
                      allow_small_or_imprecise_dtypes=True).then_inc(pool_prep, 1)
            for i in range(2):
                pool.memset(k0[i][:, :], 0.0).then_inc(pool_prep, 1)
                pool.memset(mT[i][:, :].bitcast(fp32), 0.0).then_inc(pool_prep, 1)
            pool.memset(pick[:, :, :, :], 0.0).then_inc(pool_prep, 1)
            pool.wait_ge(pool_prep, POOL_PREP - 2)
            for part in range(2):
                pool.affine_select(out=pick[:, :, :, :], in_=pick[:, :, :, :], compare_op=ALU.not_equal,
                                   fill=1.0, base=-2 * NE * part, pattern=[[-1, NE], [-NE, 2], [0, D]],
                                   channel_multiplier=1).then_inc(pool_prep, 1)
                pool.wait_ge(pool_prep, POOL_PREP - 1 + part)

            pool.wait_ge(cst_in, 16 * N_CST)

            def step_a(half, j):
                send = item(half, j, 1, PAIRS)
                it = item(half, j, 3, PAIRS)
                if it:
                    n, m, i = it
                    pool.wait_ge(h0_in[i], 16 * (m + 1))
                    pool.wait_ge(pool_prep, POOL_PREP)
                    pool.tensor_tensor(H1[:, bass.ds(n, 1), :].rearrange("p a (g d) -> p (a g) d", d=D),
                                       H0[i][:, :, :], bo_bc[0:Q, None, :].to_broadcast([Q, G, D]), ALU.add)\
                        .then_inc(hb_ok, 1)
                it = item(half, j, 4, PAIRS)
                if it:
                    n, m, i = it
                    pool.wait_ge(zhi_ok, n + 1)
                    pool.tensor_tensor(zsplit[i][:, :, 1, :], z[:, :, :], zsplit[i][:, :, 0, :], ALU.subtract)\
                        .then_inc(zlo_ok, 1)
                if send:
                    pool.wait_ge(pre, PRE * (send[0] + 1))
                    pool.wait_ge(ranked, RANK * (send[0] + 1))
                    if not first(send[0], 2):
                        pool.wait_ge(hb_ok, send[0] - 1)
                it = item(half, j, 3, PAIRS)
                if it:
                    n, m, i = it
                    if not first(n):
                        pool.wait_ge(z_ok, n)
                    pool.wait_ge(nrm, NRM * (n + 1))
                    pool.tensor_tensor(rstd[:, :], hvar_eps[:, :], neg_half[:, 0:G], ALU.pow).then_inc(rstd_ok, 1)
                if send:
                    n, m, i = send
                    for t in range(TT):
                        pool.indirect_dma_start(
                            out=h_sorted[:, :],
                            out_offset=bass.IndirectOffsetOnAxis(ap=row_of[i][:, t:t + 1], axis=0),
                            in_=h[i][:, t, :], in_offset=None).then_inc(scattered[i], 16)

            run_a(pool, step_a)

            def step_b(half, j):
                nxt, main = item(half, j, 0, UNITS), item(half, j, 2, UNITS)
                for e in range(1, NE):
                    if main:
                        n, m, i = main
                        pool.wait_ge(ye_ok, NE * n + e + 1)
                        if e > 1:
                            pool.wait_ge(acc_ok, (NE - 1) * n + e - 1)
                        pool.tensor_tensor(acc[i][:, :], acc[i][:, :], ye[e % 2][:, :], ALU.add)\
                            .then_inc(acc_ok, 1)
                    if nxt and e == 1:
                        n, m, i = nxt
                        pool.wait_ge(ln, LN * n + 4)
                        pool.tensor_tensor(urstd[:, :], uvar_eps[:, :], neg_half[:, :], ALU.pow)\
                            .then_inc(urstd_ok, 1)
                    if nxt and e == 5:
                        n, m, i = nxt
                        pool.wait_ge(uhi_ok, n + 1)
                        pool.tensor_tensor(usplit[:, :, 1, :], uz[:, :, :], usplit[:, :, 0, :], ALU.subtract)\
                            .then_inc(ulo_ok, 1)

            run_b(pool, step_b)

        @block.scalar
        def _(act):
            act.wait_ge(pe_prep, 1)
            act.activation(wqk_hi[:, :], PS[0][:, 0:2 * D], ACT.Copy).then_inc(act_prep, 1)
            act.activation(woT[:, :], PS[1][0:D, 0:D], ACT.Copy).then_inc(act_prep, 1)
            act.wait_ge(pe_prep, 2)
            act.activation(wvx_hi[:, 0:D], PS[2][:, 0:D], ACT.Copy).then_inc(act_prep, 1)
            act.activation(wvx_hi[:, D:VX], PS[0][:, 0:D + 1:D], ACT.Copy).then_inc(act_prep, 1)
            act.activation(vbias[:, 0:D], PS[2][0:Q, D:2 * D], ACT.Copy).then_inc(act_prep, 1)
            act.wait_ge(dve_prep, 5)
            act.activation(w1_hi[:, :, :], w1_g[:, :, :], ACT.Copy).then_inc(act_prep, 1)
            act.wait_ge(pool_prep, POOL_PREP)
            act.activation(wr_split[:, 0, :], wr_g[:, :], ACT.Copy).then_inc(act_prep, 1)
            act.activation(spread[:, :, :], pick[:, :, :, :].rearrange("p e c d -> p e (c d)"), ACT.Copy)\
                .then_inc(act_prep, 1)

            def step_a(half, j):
                it = item(half, j, 5, PAIRS)
                if it:
                    n, m, i = it
                    act.wait_ge(zTp_ok, n + 1)
                    if not first(n, 2):
                        act.wait_ge(qkv_ok, n - 1)
                    act.activation(zT[i][:, :], zT_ps, ACT.Copy).then_inc(zT_ok, 1)
                it = item(half, j, 4, PAIRS)
                if it:
                    n, m, i = it
                    act.wait_ge(z_ok, n + 1)
                    if not first(n, 2):
                        act.wait_ge(zTp_ok, n - 1)
                        act.wait_ge(zlo_ok, n - 1)
                    act.activation(zsplit[i][:, :, 0, :], z[:, :, :], ACT.Copy).then_inc(zhi_ok, 1)
                it = item(half, j, 3, PAIRS)
                if it:
                    n, m, i = it
                    act.wait_ge(nrm, NRM * n + 2)
                    act.activation(sq[:, :, :], hc[:, :, :], ACT.Square, scale=D ** -0.5).then_inc(sq_ok, 1)
                it = item(half, j, 7, PAIRS)
                if it:
                    n, m, i = it
                    for b in range(2):
                        act.wait_ge(ETp_ok, 2 * n + b + 1)
                        if not first(n):
                            act.wait_ge(OTp_ok, n)
                        act.activation(ET[b][:, :], ET_ps[b][0:Q, 0:R * S], ACT.Copy).then_inc(ET_ok, 1)
                it = item(half, j, 0, PAIRS)
                if it:
                    n, m, i = it
                    act.wait_ge(pre, PRE * n + 3)
                    act.activation(expneg[:, :], score[i][:, :], ACT.Exp, scale=-1.0).then_inc(expneg_ok, 1)
                it = item(half, j, 6, PAIRS)
                if it:
                    n, m, i = it
                    act.wait_ge(max_ok, MAX * (n + 1))
                    if not first(n, 2):
                        act.wait_ge(ETp_ok, 2 * (n - 1))
                        act.wait_ge(scaled, SCL * (n - 1))
                    for g in range(G):
                        last = act.activation(E[i][:, g, :], S_ps[g // R][0:Q, (g % R) * S:(g % R + 1) * S],
                                              ACT.Exp, bias=nmax[i][:, g:g + 1], scale=SCALE,
                                              accum_out=den[i][:, g:g + 1])
                    last.then_inc(exp_ok, 1)
                it = item(half, j, 5, PAIRS)
                if it:
                    n, m, i = it
                    act.wait_ge(qkv_ok, n + 1)
                    if not first(n, 2):
                        act.wait_ge(S_ok, 2 * (n - 1))
                        act.wait_ge(k0_ok, n - 1)
                    act.activation(qk[i][:, :], qk_ps, ACT.Identity, bias=bqk_col[:, 0:1]).then_inc(qk_ok, 1)
                it = item(half, j, 7, PAIRS)
                if it:
                    n, m, i = it
                    act.wait_ge(OTp_ok, n + 1)
                    if not first(n):
                        act.wait_ge(back_ok, n)
                    act.activation(OT[:, :], OT_ps, ACT.Copy).then_inc(OT_ok, 1)

            run_a(act, step_a)

            def mix_out(it, e):
                n, m, i = it
                k = NE * n + e
                act.wait_ge(mbp_ok, k + 1)
                if not first(n) or e >= 2:
                    act.wait_ge(ye_ok, k - 1)
                act.activation(mb[e % 2][:, :], mb_ps[:, 0:C], ACT.Copy).then_inc(mb_ok, 1)

            def step_b(half, j):
                nxt, prep, main, prev = (item(half, j, lag, UNITS) for lag in range(4))
                for e in range(NE):
                    if main and e >= 1:
                        mix_out(main, e - 1)
                    if prev and e == 0:
                        mix_out(prev, NE - 1)
                    if nxt and e == 2:
                        n, m, i = nxt
                        act.wait_ge(ln, LN * n + 2)
                        act.activation(usq[:, :, :], uc[:, :, :], ACT.Square, scale=((1.0 + EPS) / D) ** 0.5)\
                            .then_inc(usq_ok, 1)
                    if main:
                        n, m, i = main
                        k = NE * n + e
                        for c in range(2):
                            act.wait_ge(hidp_ok, 2 * k + c + 1)
                            if not first(n) or e >= 2:
                                act.wait_ge(yp_ok, k - 1)
                            act.activation(hid[e % 2][c][:, :], hid_ps[e % 2][c][:, 0:C], ACT.Gelu,
                                           bias=b1_eff[:, e:e + 1]).then_inc(hid_ok, 1)
                    if prep and e < 2:
                        n, m, i = prep
                        act.wait_ge(uTp_ok, 2 * n + e + 1)
                        act.activation(uT[i][e][:, :], aux_ps[:, 0:C], ACT.Copy).then_inc(uT_ok, 1)
                    if main and e == 0:
                        n, m, i = main
                        act.wait_ge(mTp_ok, n + 1)
                        act.activation(mT[i][0:4 * NE, :], mb_ps[0:4 * NE, 0:C], ACT.Copy).then_inc(mT_ok, 1)
                    if prep and e == 5:
                        n, m, i = prep
                        act.wait_ge(top, TOP * n + 15)
                        act.activation(tanh[:, :], gap[:, :], ACT.Tanh, scale=0.5).then_inc(tanh_ok, 1)
                    if nxt and e == 6:
                        n, m, i = nxt
                        act.wait_ge(ln, LN * (n + 1))
                        if not first(n):
                            act.wait_ge(uTp_ok, 2 * n)
                        act.activation(usplit[:, :, 0, :], uz[:, :, :], ACT.Copy).then_inc(uhi_ok, 1)

            run_b(act, step_b)

        @block.tensor
        def _(pe):
            pe.wait_ge(pool_prep, 5)
            pe.wait_ge(attn_in, 16 * N_ATTN)
            pe.transpose(PS[0][:, 0:D], wqk_nat[:, 0:2, :].rearrange("o c d -> o (c d)"), ident[0:D, 0:D])
            pe.transpose(PS[0][:, D:2 * D], wqk_nat[:, 2:4, :].rearrange("o c d -> o (c d)"), ident[0:D, 0:D])
            pe.transpose(PS[1][0:D, 0:D], wo_nat[:, :], ident[0:D, 0:D]).then_inc(pe_prep, 1)
            pe.wait_ge(act_prep, 2)
            pe.matmul(PS[2][:, 0:D], wv_nat[:, :, :].rearrange("o c d -> o (c d)"), woT[:, :], start=True, stop=True)
            pe.matmul(PS[2][0:Q, D:2 * D], bv_col[:, 0:1].to_broadcast([D, Q]), woT[:, :],
                      start=True, stop=True).then_inc(pe_prep, 1)
            pe.wait_ge(ffn_in, 16 * N_FFN)
            pe.wait_ge(w1_in, 16 * (N_W1 + 1))
            for e in range(NE):
                pe.matmul(PS[3][:, e:e + 1], w1_raw[0:D, e, :], beta_col[:, :], start=True, stop=True)
            pe.matmul(PS[3][0:Q, 3 * NE:4 * NE], beta_col[:, 0:1].to_broadcast([D, Q]), wr_raw[0:D, :],
                      start=True, stop=True)
            pe.transpose(PS[3][:, NE:2 * NE], b1_nat[:, :], ident[0:NE, 0:NE])
            pe.transpose(PS[3][:, 2 * NE:3 * NE], b2_nat[:, :], ident[0:NE, 0:NE]).then_inc(pe_prep, 1)
            pe.wait_ge(act_prep, 5)
            pe.wait_ge(dve_prep, DVE_PREP_PSUM)

            def step_a(half, j):
                it = item(half, j, 6, PAIRS)
                if it:
                    n, m, i = it
                    pe.wait_ge(qk_ok, n + 1)
                    pe.wait_ge(k0_ok, n + 1)
                    if not first(n):
                        pe.wait_ge(exp_ok, n)
                    for b in range(2):
                        for qt in range(R):
                            c0 = b * S + qt * Q
                            last = pe.matmul(S_ps[b][0:Q, qt * S:(qt + 1) * S], qk[i][:, c0:c0 + Q],
                                             k0[i][:, b * S:(b + 1) * S], start=True, stop=True)
                        last.then_inc(S_ok, 1)
                beats, project = item(half, j, 1, PAIRS), item(half, j, 5, PAIRS)
                if beats:
                    n, m, i = beats
                    pe.wait_ge(cmp_ok, CMP * (n + 1))
                    v_before = item(half, j, 6, PAIRS)
                    if v_before:
                        pe.wait_ge(v_ok, v_before[0] + 1)
                    for b in range(2):
                        for t in range(T):
                            col = csum_ps[:, T * b + t:T * b + t + 1]
                            for a in range(t + 1):
                                c0 = a * T * P + (t - a) * P
                                last = pe.matmul(col, greater[:, b, c0:c0 + P], ones_bf[:, :],
                                                 start=(a == 0), stop=(a == t))
                    last.then_inc(csum_ok, 1)
                if project:
                    n, m, i = project
                    pe.wait_ge(zlo_ok, n + 1)
                    if not first(n):
                        pe.wait_ge(zT_ok, n)
                    for g in range(G):
                        last = pe.transpose(zT_ps[:, g * Q:(g + 1) * Q],
                                            zsplit[i][:, g, :, :].rearrange("p c d -> p (c d)").bitcast(fp32),
                                            ident[0:Q, 0:Q])
                    last.then_inc(zTp_ok, 1)
                it = item(half, j, 7, PAIRS)
                if it:
                    n, m, i = it
                    pe.wait_ge(exp_ok, n + 1)
                    if not first(n):
                        pe.wait_ge(OT_ok, n)
                    for b in range(2):
                        if b == 1 and not first(n):
                            pe.wait_ge(h1_ok, FIN * (n - 1) + 1)
                        for kt in range(R):
                            for qt in range(R):
                                last = pe.transpose(ET_ps[b][0:Q, kt * S + qt * Q:kt * S + (qt + 1) * Q],
                                                    E[i][:, R * b + qt, kt * Q:(kt + 1) * Q], ident[0:Q, 0:Q])
                        last.then_inc(ETp_ok, 1)
                if project:
                    n, m, i = project
                    pe.wait_ge(zT_ok, n + 1)
                    if not first(n):
                        pe.wait_ge(qk_ok, n)
                        pe.wait_ge(v_ok, n)
                    if beats:
                        pe.wait_ge(ranked, RANK * beats[0] + 1)
                    pe.matmul(qk_ps, wqk_hi[:, :], zT[i][:, :], start=True, stop=False)
                    pe.matmul(qk_ps, wqk_lo[:, :], zT[i][:, :], start=False, stop=True)
                    for g in range(G):
                        for w in (wvx_hi, wvx_lo):
                            last = pe.matmul(v_ps[:, g * VX:(g + 1) * VX], zT[i][:, g * Q:(g + 1) * Q], w[:, :],
                                             start=(w is wvx_hi), stop=(w is wvx_lo))
                    last.then_inc(qkv_ok, 1)
                it = item(half, j, 7, PAIRS)
                if it:
                    n, m, i = it
                    pe.wait_ge(v_ok, n + 1)
                    for b in range(2):
                        pe.wait_ge(ET_ok, 2 * n + b + 1)
                        for kt in range(R):
                            last = pe.matmul(OT_ps[b * D:(b + 1) * D, :], v[i][:, R * b + kt, 0:D],
                                             ET[b][:, kt * S:(kt + 1) * S], start=(kt == 0), stop=(kt == R - 1))
                    last.then_inc(OTp_ok, 1)
                it = item(half, j, 0, PAIRS)
                if it:
                    n, m, i = it
                    pe.wait_ge(pre, PRE * n + 3)
                    if not first(n):
                        pe.wait_ge(cmp_ok, CMP * n)
                    for t in range(TT):
                        last = pe.transpose(srow[:, t * P:(t + 1) * P],
                                            score[i][:, t:t + 1].to_broadcast([P, P]), ident[:, :])
                    last.then_inc(srow_ok, 1)
                it = item(half, j, 7, PAIRS)
                if it:
                    n, m, i = it
                    pe.wait_ge(OT_ok, n + 1)
                    pe.wait_ge(ET_ok, 2 * (n + 1))
                    for r in range(R):
                        last = pe.transpose(back_ps[:, r * P:(r + 1) * P], OT[:, r * Q:(r + 1) * Q], ident[:, :])
                    last.then_inc(back_ok, 1)

            run_a(pe, step_a)
            pe.wait_ge(h1_ok, FIN * PAIRS)
            pe.wait_ge(act_prep, ACT_PREP)
            pe.wait_ge(dve_prep, DVE_PREP)

            def step_b(half, j):
                prep, main, prev = (item(half, j, lag, UNITS) for lag in range(1, 4))
                for e in range(NE):
                    late, f = (main, e - 1) if e else (prev, NE - 1)
                    if late:
                        n, m, i = late
                        k = NE * n + f
                        if f == 0:
                            pe.wait_ge(mT_ok, n + 1)
                        if not first(n) or f:
                            pe.wait_ge(mb_ok, k)
                        pe.matmul(mb_ps[:, 0:C], spread[:, f, :], mT[i][:, :], start=True, stop=True)\
                            .then_inc(mbp_ok, 1)
                    if main:
                        n, m, i = main
                        k = NE * n + e
                        if not first(n) or e >= 2:
                            pe.wait_ge(hid_ok, 2 * (k - 1))
                        for w in (w1_hi, w1_lo):
                            for c in range(2):
                                last = pe.matmul(hid_ps[e % 2][c][:, 0:C], w[:, e, :], uT[i][c][:, :],
                                                 start=(w is w1_hi), stop=(w is w1_lo))
                                if w is w1_lo:
                                    last.then_inc(hidp_ok, 1)
                    if prep and 2 <= e < 4:
                        n, m, i = prep
                        c = e - 2
                        pe.wait_ge(uT_ok, 2 * n + c + 1)
                        if main:
                            if not first(main[0]) or f >= 2:
                                pe.wait_ge(ye_ok, NE * main[0] + f - 1)
                        for g in range(G):
                            last = pe.matmul(y_ps[f % 2][0:Q, C + 2 * NE * g:C + 2 * NE * (g + 1)],
                                             uT[i][c][:, g * Q:(g + 1) * Q],
                                             wr_split[:, :, :].rearrange("p a e -> p (a e)"), start=True, stop=True)
                        last.then_inc(lgp_ok, 1)
                    if late:
                        n, m, i = late
                        k = NE * n + f
                        if not first(n) or f >= 2:
                            pe.wait_ge(ye_ok, k - 1)
                        if prep and 4 <= e < 6:
                            pe.wait_ge(top, TOP * prep[0] + 2 * (e - 3))
                        for c in range(2):
                            pe.wait_ge(hid_ok, 2 * k + c + 1)
                            last = pe.matmul(y_ps[f % 2][c * D:(c + 1) * D, 0:C], w2_sb[:, f, :],
                                             hid[f % 2][c][:, :], start=True, stop=True)
                        last.then_inc(yp_ok, 1)
                    if main and e == 0:
                        n, m, i = main
                        pe.wait_ge(top, TOP * (n + 1))
                        if not first(n):
                            pe.wait_ge(mb_ok, NE * n)
                        for g in range(G):
                            last = pe.transpose(
                                mb_ps[0:4 * NE, g * Q:(g + 1) * Q],
                                msplit[:, g, :, :, :].rearrange("p a c e -> p (a c e)").bitcast(fp32),
                                ident[0:Q, 0:Q])
                        last.then_inc(mTp_ok, 1)
                    if prep and e < 2:
                        n, m, i = prep
                        if e == 0:
                            pe.wait_ge(ulo_ok, n + 1)
                            if not first(n, 3):
                                pe.wait_ge(y_ok, n - 2)
                        else:
                            pe.wait_ge(uT_ok, 2 * n + 1)
                        for g in range(G):
                            last = pe.transpose(aux_ps[:, g * Q:(g + 1) * Q],
                                                usplit[:, G * e + g, :, :].rearrange("p c d -> p (c d)").bitcast(fp32),
                                                ident[0:Q, 0:Q])
                        last.then_inc(uTp_ok, 1)
                    if prev and e == 4:
                        n, m, i = prev
                        pe.wait_ge(acc_ok, (NE - 1) * (n + 1))
                        if prep:
                            pe.wait_ge(uT_ok, 2 * (prep[0] + 1))
                        for g in range(G):
                            last = pe.transpose(aux_ps[0:Q, g * P:(g + 1) * P], acc[i][:, g * Q:(g + 1) * Q],
                                                ident[:, :])
                        last.then_inc(backB_ok, 1)

            run_b(pe, step_b)

        @block.vector
        def _(dve):
            dve.wait_ge(act_prep, 5)
            dve.tensor_tensor(wqk_lo[:, :], PS[0][:, 0:2 * D], wqk_hi[:, :], ALU.subtract).then_inc(dve_prep, 1)
            dve.tensor_tensor(wvx_lo[:, 0:D], PS[2][:, 0:D], wvx_hi[:, 0:D], ALU.subtract).then_inc(dve_prep, 1)
            dve.tensor_tensor(wvx_lo[:, D:VX], PS[0][:, 0:D + 1:D], wvx_hi[:, D:VX], ALU.subtract)\
                .then_inc(dve_prep, 1)
            dve.wait_ge(ffn_in, 16 * N_FFN)
            dve.wait_ge(w1_in, 16 * (N_W1 + 1))
            dve.tensor_scalar(w1_g[:, :, :], w1_raw[:, :, :], gamma_col[:, 0:1], None, ALU.mult)\
                .then_inc(dve_prep, 1)
            dve.tensor_scalar(wr_g[:, :], wr_raw[:, :], gamma_col[:, 0:1], None, ALU.mult).then_inc(dve_prep, 1)
            dve.wait_ge(pe_prep, 3)
            dve.tensor_copy(b1_T[:, :], PS[3][:, NE:2 * NE]).then_inc(dve_prep, 1)
            dve.tensor_copy(b2_col[:, :], PS[3][:, 2 * NE:3 * NE]).then_inc(dve_prep, 1)
            dve.wait_ge(dve_prep, 6)
            dve.tensor_tensor(b1_eff[:, :], PS[3][:, 0:NE], b1_T[:, :], ALU.add).then_inc(dve_prep, 1)
            dve.tensor_tensor(br_eff[:, :], PS[3][0:Q, 3 * NE:4 * NE], br_bc[:, :], ALU.add).then_inc(dve_prep, 1)
            dve.wait_ge(act_prep, ACT_PREP)
            dve.tensor_tensor(w1_lo[:, :, :], w1_g[:, :, :], w1_hi[:, :, :], ALU.subtract).then_inc(dve_prep, 1)
            dve.tensor_tensor(wr_split[:, 1, :], wr_g[:, :], wr_split[:, 0, :], ALU.subtract).then_inc(dve_prep, 1)
            dve.wait_ge(cst_in, 16 * N_CST)

            def score_products(n, m, i):
                if isinstance(n, int) and n < 3:
                    dve.wait_ge(x_in[n], 16)
                elif isinstance(n, int) and n == 3:
                    dve.wait_ge(x_in[3], 16)
                dve.tensor_tensor(xw[:, :].rearrange("p (t d) -> p t d", d=D), X[:, bass.ds(TT * n, TT), :],
                                  w_bc[:, None, :].to_broadcast([P, TT, D]), ALU.mult).then_inc(pre, 1)

            def score_sum(n, m, i):
                dve.wait_ge(pre, PRE * n + 1)
                dve.tensor_reduce(ssum[:, :], xw[:, :].rearrange("p (t d) -> p t d", d=D), AX.X, ALU.add)\
                    .then_inc(pre, 1)

            def score_bias(n, m, i):
                dve.wait_ge(pre, PRE * n + 2)
                dve.tensor_scalar(score[i][:, :], ssum[:, :], b_col[:, 0:1], None, ALU.add).then_inc(pre, 1)

            def gate_one_plus(n, m, i):
                dve.wait_ge(expneg_ok, n + 1)
                dve.tensor_scalar(gate1[:, :], expneg[:, :], 1.0, None, ALU.add).then_inc(pre, 1)

            def gate_value(n, m, i):
                dve.wait_ge(pre, PRE * n + 4)
                dve.reciprocal(gate[:, :], gate1[:, :]).then_inc(pre, 1)

            def gated(n, m, i):
                dve.wait_ge(pre, PRE * n + 5)
                if not first(n, 2):
                    dve.wait_ge(scattered[i], 16 * TT * m)
                dve.tensor_tensor(h[i][:, :, :], X[:, bass.ds(TT * n, TT), :],
                                  gate[:, :, None].to_broadcast([P, TT, D]), ALU.mult).then_inc(pre, 1)

            def compare(n, m, i):
                dve.wait_ge(srow_ok, n + 1)
                if not first(n):
                    dve.wait_ge(csum_ok, n)
                    dve.wait_ge(ranked, RANK * n)
                for b in range(2):
                    for t in range(T):
                        c0, w = t * T * P, (T - t) * P
                        g = T * b + t
                        dve.scalar_tensor_tensor(
                            out=greater[:, b, c0:c0 + w], in0=srow[:, (g * P):(T * b + T) * P],
                            scalar=score[i][:, g:g + 1], in1=later[:, 0:w], op0=ALU.is_gt, op1=ALU.mult,
                            accum_out=rowsum[:, g:g + 1]).then_inc(cmp_ok, 1)

            def rank_less_index(n, m, i):
                dve.wait_ge(csum_ok, n + 1)
                dve.wait_ge(cmp_ok, CMP * (n + 1))
                dve.tensor_tensor(ahead[:, :], rowsum[:, :], csum_ps, ALU.subtract).then_inc(ranked, 1)

            def rank_row(n, m, i):
                dve.wait_ge(ranked, RANK * n + 1)
                if not first(n, 2):
                    dve.wait_ge(scattered[i], 16 * TT * m)
                dve.tensor_tensor(row_of[i][:, :], ahead[:, :], row_index[:, bass.ds(TT * n, TT)], ALU.add)\
                    .then_inc(ranked, 1)

            def norm_sum(n, m, i):
                dve.wait_ge(h0_in[i], 16 * (m + 1))
                dve.tensor_reduce(hsum[:, :], H0[i][:, :, :], AX.X, ALU.add).then_inc(nrm, 1)

            def norm_center(n, m, i):
                dve.wait_ge(nrm, NRM * n + 1)
                dve.scalar_tensor_tensor(out=hc[:, :, :], in0=hsum[:, :, None].to_broadcast([Q, G, D]),
                                         scalar=1.0 / D, in1=H0[i][:, :, :], op0=ALU.mult, op1=ALU.subtract)\
                    .then_inc(nrm, 1)

            def norm_var(n, m, i):
                dve.wait_ge(sq_ok, n + 1)
                dve.tensor_reduce(hvar[:, :], sq[:, :, :], AX.X, ALU.add).then_inc(nrm, 1)

            def norm_var_eps(n, m, i):
                dve.wait_ge(nrm, NRM * n + 3)
                dve.tensor_scalar(hvar_eps[:, :], hvar[:, :], EPS, None, ALU.add).then_inc(nrm, 1)

            def norm_z(n, m, i):
                dve.wait_ge(rstd_ok, n + 1)
                if not first(n):
                    dve.wait_ge(zlo_ok, n)
                dve.scalar_tensor_tensor(out=z[:, :, :], in0=hc[:, :, :], scalar=-1.0,
                                         in1=rstd[:, :, None].to_broadcast([Q, G, D]), op0=ALU.mult, op1=ALU.mult)\
                    .then_inc(z_ok, 1)

            def values(n, m, i):
                dve.wait_ge(qkv_ok, n + 1)
                if not first(n, 2):
                    dve.wait_ge(OTp_ok, n - 1)
                dve.tensor_tensor(v[i][:, :, :], v_ps.rearrange("p (g c) -> p g c", g=G),
                                  vbias[:, None, :].to_broadcast([Q, G, VX]), ALU.add).then_inc(v_ok, 1)

            def keys(n, m, i):
                dve.wait_ge(qk_ok, n + 1)
                if not first(n, 2):
                    dve.wait_ge(S_ok, 2 * (n - 1))
                dve.tensor_copy(k0[i][0:D, :], qk[i][D:P, :]).then_inc(k0_ok, 1)

            def row_max(n, m, i, b):
                dve.wait_ge(S_ok, 2 * n + b + 1)
                dve.tensor_reduce(smax[:, R * b:R * (b + 1)],
                                  S_ps[b][0:Q, 0:R * S].rearrange("p (r s) -> p r s", r=R), AX.X, ALU.max)\
                    .then_inc(max_ok, 1)

            def row_max_0(n, m, i):
                row_max(n, m, i, 0)

            def row_max_1(n, m, i):
                row_max(n, m, i, 1)

            def minus_max(n, m, i):
                dve.wait_ge(max_ok, MAX * n + 2)
                if not first(n, 2):
                    dve.wait_ge(exp_ok, n - 1)
                dve.tensor_scalar(nmax[i][:, :], smax[:, :], -SCALE, None, ALU.mult).then_inc(max_ok, 1)

            def one_over_den(n, m, i):
                dve.wait_ge(exp_ok, n + 1)
                dve.reciprocal(rden[:, :], den[i][:, :]).then_inc(scaled, 1)

            def mask_q(n, m, i):
                dve.wait_ge(scaled, SCL * n + 1)
                dve.wait_ge(v_ok, n + 1)
                dve.scalar_tensor_tensor(out=rden_q[:, :], in0=v[i][:, :, D], scalar=0.0, in1=rden[:, :],
                                         op0=ALU.not_equal, op1=ALU.mult).then_inc(scaled, 1)

            def mask_k(n, m, i):
                dve.wait_ge(scaled, SCL * n + 2)
                dve.scalar_tensor_tensor(out=rden_qk[i][:, :], in0=v[i][:, :, D + 1], scalar=0.0, in1=rden_q[:, :],
                                         op0=ALU.not_equal, op1=ALU.mult).then_inc(scaled, 1)

            def attention(n, m, i):
                dve.wait_ge(scaled, SCL * (n + 1))
                dve.wait_ge(back_ok, n + 1)
                for b in range(2):
                    last = dve.tensor_tensor(
                        attn[:, b, :, :], back_ps.rearrange("p (r b d) -> p b r d", r=R, b=2)[:, b, :, :],
                        rden_qk[i][:, R * b:R * (b + 1), None].to_broadcast([Q, R, D]), ALU.mult)
                last.then_inc(h1_ok, 1)

            def residual(n, m, i):
                dve.wait_ge(hb_ok, n + 1)
                dve.wait_ge(h1_ok, FIN * n + 1)
                H1n = H1[:, bass.ds(n, 1), :].rearrange("p a f -> p (a f)")
                dve.tensor_tensor(H1n, attn[:, :, :, :].rearrange("p b r d -> p (b r d)"), H1n, ALU.add)\
                    .then_inc(h1_ok, 1)

            def step_a(half, j):
                for stage, lag in (
                        (attention, 8), (norm_z, 4), (compare, 1), (residual, 8),
                        (score_products, 0), (norm_sum, 3), (score_sum, 0), (norm_center, 3),
                        (score_bias, 0), (one_over_den, 7), (row_max_0, 6), (rank_less_index, 1), (mask_q, 7),
                        (row_max_1, 6), (rank_row, 1), (mask_k, 7), (minus_max, 6), (gate_one_plus, 0),
                        (norm_var, 3), (gate_value, 0), (norm_var_eps, 3), (gated, 0), (keys, 5), (values, 5)):
                    it = item(half, j, lag, PAIRS)
                    if it:
                        stage(*it)

            dve.wait_ge(pool_prep, POOL_PREP)
            run_a(dve, step_a)

            def norm(it, part):
                n, m, i = it
                rows = H1[:, bass.ds(2 * n, 2), :].rearrange("p c (g d) -> p (c g) d", d=D)
                if part == 0:
                    dve.tensor_reduce(usum[:, :], rows, AX.X, ALU.add).then_inc(ln, 1)
                    dve.wait_ge(ln, LN * n + 1)
                    dve.scalar_tensor_tensor(out=uc[:, :, :], in0=usum[:, :, None].to_broadcast([Q, TU, D]),
                                             scalar=1.0 / D, in1=rows, op0=ALU.mult, op1=ALU.subtract)\
                        .then_inc(ln, 1)
                if part == 1:
                    dve.wait_ge(usq_ok, n + 1)
                    dve.tensor_reduce(uvar[:, :], usq[:, :, :], AX.X, ALU.add).then_inc(ln, 1)
                    dve.wait_ge(ln, LN * n + 3)
                    dve.tensor_scalar(uvar_eps[:, :], uvar[:, :], EPS * EPS, None, ALU.add).then_inc(ln, 1)
                if part == 2:
                    dve.wait_ge(urstd_ok, n + 1)
                    if not first(n):
                        dve.wait_ge(ulo_ok, n)
                    dve.scalar_tensor_tensor(out=uz[:, :, :], in0=uc[:, :, :], scalar=-1.0,
                                             in1=urstd[:, :, None].to_broadcast([Q, TU, D]),
                                             op0=ALU.mult, op1=ALU.mult).then_inc(ln, 1)

            def largest(done, src, top_, is_, pr_, pm_):
                dve.tensor_reduce(top_[:, :], src[:, :, :], AX.X, ALU.max).then_inc(top, 1)
                dve.wait_ge(top, done + 1)
                dve.tensor_tensor(is_[:, :, :], src[:, :, :], top_[:, :, None].to_broadcast([Q, TU, NE]),
                                  ALU.is_equal).then_inc(top, 1)
                dve.wait_ge(top, done + 2)
                dve.tensor_tensor(pr_[:, :, :], is_[:, :, :], falling[:, None, :].to_broadcast([Q, TU, NE]),
                                  ALU.mult).then_inc(top, 1)
                dve.wait_ge(top, done + 3)
                dve.tensor_reduce(pm_[:, :], pr_[:, :, :], AX.X, ALU.max).then_inc(top, 1)

            def route(it, part):
                n, m, i = it

                def bc(a):
                    return a[:, :, None].to_broadcast([Q, TU, NE])

                def flat(a):
                    return a[:, :, :].rearrange("p g e -> p (g e)")
                if part < 2:
                    tiles = slice(G * part, G * (part + 1))
                    parts = y_ps[1 - part][0:Q, C:C + 2 * NE * G].rearrange("p (g a e) -> p g a e", g=G, a=2)
                    dve.wait_ge(lgp_ok, 2 * n + part + 1)
                    dve.tensor_tensor(lg_hi[:, tiles, :], parts[:, :, 0, :],
                                      br_eff[:, None, :].to_broadcast([Q, G, NE]), ALU.add).then_inc(top, 1)
                    dve.wait_ge(top, TOP * n + 2 * part + 1)
                    dve.tensor_tensor(lg[:, tiles, :], parts[:, :, 1, :], lg_hi[:, tiles, :], ALU.add)\
                        .then_inc(top, 1)
                if part == 2:
                    dve.wait_ge(top, TOP * n + 4)
                    largest(TOP * n + 4, lg, top1, is1, pr1, pm1)
                if part == 3:
                    dve.wait_ge(top, TOP * n + 8)
                    dve.tensor_tensor(sel1[:, :, :], pr1[:, :, :], bc(pm1), ALU.is_equal).then_inc(top, 1)
                    dve.wait_ge(top, TOP * n + 9)
                    dve.scalar_tensor_tensor(out=flat(lg2), in0=flat(sel1), scalar=-3e38, in1=flat(lg),
                                             op0=ALU.mult, op1=ALU.add).then_inc(top, 1)
                    dve.wait_ge(top, TOP * n + 10)
                    largest(TOP * n + 10, lg2, top2, is2, pr2, pm2)
                    dve.tensor_tensor(gap[:, :], top1[:, :], top2[:, :], ALU.subtract).then_inc(top, 1)
                if part == 4:
                    dve.wait_ge(top, TOP * n + 15)
                    dve.tensor_tensor(sel2[:, :, :], pr2[:, :, :], bc(pm2), ALU.is_equal).then_inc(top, 1)
                if part == 5:
                    dve.wait_ge(tanh_ok, n + 1)
                    dve.tensor_scalar(wt1[:, :], tanh[:, :], 0.5, 0.5, ALU.mult, ALU.add).then_inc(top, 1)
                    dve.tensor_scalar(wt2[:, :], tanh[:, :], -0.5, 0.5, ALU.mult, ALU.add).then_inc(top, 1)
                    dve.wait_ge(top, TOP * n + 18)
                    dve.tensor_tensor(mix1[:, :, :], sel1[:, :, :], bc(wt1), ALU.mult).then_inc(top, 1)
                    dve.tensor_tensor(mix2[:, :, :], sel2[:, :, :], bc(wt2), ALU.mult).then_inc(top, 1)
                    dve.wait_ge(top, TOP * n + 20)
                    dve.tensor_tensor(mix[:, :, :], mix1[:, :, :], mix2[:, :, :], ALU.add).then_inc(top, 1)
                    dve.wait_ge(top, TOP * n + 21)
                    if not first(n):
                        dve.wait_ge(mTp_ok, n)
                    for c in range(2):
                        last = dve.tensor_copy(msplit[:, :, 0, c, :], mix[:, G * c:G * (c + 1), :])
                    last.then_inc(top, 1)
                    dve.wait_ge(top, TOP * n + 22)
                    for c in range(2):
                        last = dve.tensor_tensor(msplit[:, :, 1, c, :], mix[:, G * c:G * (c + 1), :],
                                                 msplit[:, :, 0, c, :], ALU.subtract)
                    last.then_inc(top, 1)

            def step_b(half, j):
                nxt, prep, main, fin = (item(half, j, lag, UNITS) for lag in range(4))
                for e in range(NE):
                    if main:
                        n, m, i = main
                        k = NE * n + e
                        dve.wait_ge(yp_ok, k + 1)
                        dve.wait_ge(mb_ok, k + 1)
                        if e == 0:
                            if not first(n, 2):
                                dve.wait_ge(backB_ok, n - 1)
                        elif not first(n) or e > 2:
                            dve.wait_ge(acc_ok, (NE - 1) * n + max(e - 2, 0))
                        dst = ye[e % 2] if e else acc[i]
                        dve.scalar_tensor_tensor(out=dst[:, :], in0=y_ps[e % 2][:, 0:C], scalar=b2_col[:, e:e + 1],
                                                 in1=mb[e % 2][:, :], op0=ALU.add, op1=ALU.mult).then_inc(ye_ok, 1)
                    if prep and e == 1:
                        route(prep, 0)
                    if nxt and e < 2:
                        norm(nxt, e)
                    if prep and e == 2:
                        route(prep, 1)
                        route(prep, 2)
                    if prep and e == 3:
                        route(prep, 3)
                    if nxt and e == 4:
                        norm(nxt, 2)
                    if prep and e == 4:
                        route(prep, 4)
                    if prep and e == 5:
                        route(prep, 5)
                    if fin and e == 6:
                        n, m, i = fin
                        dve.wait_ge(backB_ok, n + 1)
                        for c in range(2):
                            last = dve.tensor_tensor(
                                y[:, bass.ds(2 * n + c, 1), :, :].rearrange("p a g d -> p (a g) d"), aux_ps[0:Q, :].rearrange("p (g c d) -> p c g d", g=G, c=2)[:, c],
                                H1[:, bass.ds(2 * n + c, 1), :].rearrange("p a (g d) -> p (a g) d", d=D), ALU.add)
                        last.then_inc(y_ok, 1)

            run_b(dve, step_b)


POOL_PREP = 8 + 4 + 1 + 2
ACT_PREP = 8
DVE_PREP_PSUM = 9
DVE_PREP = 11

_INS = ['x', 'L0_tok_w', 'L0_tok_b', 'L0_attn_Wq', 'L0_attn_bq', 'L0_attn_Wk', 'L0_attn_bk', 'L0_attn_Wv',
        'L0_attn_bv', 'L0_attn_Wo', 'L0_attn_bo', 'L0_ffn_gamma', 'L0_ffn_beta', 'L0_ffn_Wr', 'L0_ffn_br',
        'L0_ffn_W1', 'L0_ffn_b1', 'L0_ffn_W2', 'L0_ffn_b2']
KEPT = 0.8


def kernel(**inputs):
    import numpy as _np
    import concourse.bacc as _bacc
    from concourse import mybir as _mybir
    from concourse.bass_utils import run_bass_kernel_spmd as _run

    nc = _bacc.Bacc("TRN2", target_bir_lowering=False, num_devices=1)
    arrays, args = {}, []
    for name in _INS:
        a = _np.ascontiguousarray(inputs[name])
        arrays[f"in_{name}"] = a
        args.append(nc.dram_tensor(f"in_{name}", a.shape, _mybir.dt.from_np(a.dtype), kind="ExternalInput").ap())
    b, n, d = inputs['x'].shape
    args.append(nc.dram_tensor("out_0", (b, max(1, int(n * KEPT)), d), _mybir.dt.float32, kind="ExternalOutput").ap())
    audio_tower_kernel(nc, *args)
    r = _run(nc, [arrays], core_ids=[0])
    return r.results[0]["out_0"]
```

```python
import concourse.bass as bass
from concourse import mybir
from concourse.alu_op_type import AluOpType as ALU
from contextlib import ExitStack


def audio_tower_kernel(
    nc: bass.Bass,
    x: bass.AP,
    tok_w: bass.AP,
    tok_b: bass.AP,
    Wq: bass.AP,
    bq: bass.AP,
    Wk: bass.AP,
    bk: bass.AP,
    Wv: bass.AP,
    bv: bass.AP,
    Wo: bass.AP,
    bo: bass.AP,
    gamma: bass.AP,
    beta: bass.AP,
    Wr: bass.AP,
    br: bass.AP,
    W1: bass.AP,
    b1: bass.AP,
    W2: bass.AP,
    b2: bass.AP,
    out: bass.AP,
):
    fp32 = mybir.dt.float32
    fp32r = mybir.dt.float32r
    bf16 = mybir.dt.bfloat16
    i32 = mybir.dt.int32
    ACT = mybir.ActivationFunctionType
    AX = mybir.AxisListType

    B, N, D = x.shape
    S = out.shape[1]
    P = 128
    T = N // P
    R = 2
    Q = S // R
    NE, HID = W1.shape[0], W1.shape[2]
    PAIRS = B // 2
    UNITS = PAIRS // 2
    TT = 2 * T
    G = 2 * R
    TU = 2 * G
    C = 2 * S
    VX = D + 2
    SCALE = float(D) ** -0.5
    EPS = 1e-5

    x_tiles = x.rearrange("b (t p) d -> p (b t) d", p=P)
    h_sorted = nc.dram_tensor("h_sorted", (B * N, D), fp32).ap()
    h_rows = h_sorted.rearrange("(b n) d -> b n d", b=B)[:, 0:S, :].rearrange("b (p r) d -> p b (r d)", r=R)
    out_rows = out.rearrange("b (p r) d -> p b (r d)", r=R)

    ctx = ExitStack()
    with ctx:
        def sb(name, shape, dt=fp32):
            return ctx.enter_context(nc.sbuf_tensor(name, shape, dt))

        def sem(name):
            return ctx.enter_context(nc.semaphore(name))

        ident = sb("ident", [P, P])
        later = sb("later", [P, T * P])
        ones_bf = sb("ones_bf", [P, 1], bf16)
        row_index = sb("row_index", [P, B * T])
        neg_half = sb("neg_half", [Q, TU])
        falling = sb("falling", [Q, NE])
        w_bc = sb("w_bc", [P, D])
        b_col = sb("b_col", [P, 1])
        bo_bc = sb("bo_bc", [P, D])
        wqk_nat = sb("wqk_nat", [D, 4, D])
        wv_nat = sb("wv_nat", [D, 2, D])
        wo_nat = sb("wo_nat", [D, D])
        woT = sb("woT", [D, D])
        bqk_col = sb("bqk_col", [P, 1])
        bv_col = sb("bv_col", [D, 1])
        wqk_hi = sb("wqk_hi", [P, 2 * D], fp32r)
        wqk_lo = sb("wqk_lo", [P, 2 * D], fp32r)
        wvx_hi = sb("wvx_hi", [P, VX], fp32r)
        wvx_lo = sb("wvx_lo", [P, VX], fp32r)
        vbias = sb("vbias", [Q, VX])
        gamma_col = sb("gamma_col", [P, 1])
        beta_col = sb("beta_col", [D, 1])
        wr_raw = sb("wr_raw", [P, NE])
        wr_g = sb("wr_g", [P, NE])
        wr_split = sb("wr_split", [P, 2, NE], fp32r)
        br_bc = sb("br_bc", [Q, NE])
        br_eff = sb("br_eff", [Q, NE])
        w1_raw = sb("w1_raw", [P, NE, HID])
        w1_g = sb("w1_g", [P, NE, HID])
        w1_hi = sb("w1_hi", [P, NE, HID], fp32r)
        w1_lo = sb("w1_lo", [P, NE, HID], fp32r)
        b1_nat = sb("b1_nat", [NE, HID])
        b1_T = sb("b1_T", [HID, NE])
        b1_eff = sb("b1_eff", [HID, NE])
        w2_sb = sb("w2_sb", [HID, NE, D])
        b2_nat = sb("b2_nat", [NE, 2 * D])
        b2_col = sb("b2_col", [P, NE])
        pick = sb("pick", [P, NE, 2, D])
        spread = sb("spread", [P, NE, P], fp32r)

        X = sb("X", [P, B * T, D])
        H1 = sb("H1", [Q, PAIRS, G * D])
        xw = sb("xw", [P, TT, D])
        ssum = sb("ssum", [P, TT])
        score = [sb(f"score{i}", [P, TT]) for i in range(2)]
        expneg = sb("expneg", [P, TT])
        gate1 = sb("gate1", [P, TT])
        gate = sb("gate", [P, TT])
        h = [sb(f"h{i}", [P, TT, D]) for i in range(2)]
        greater = sb("greater", [P, 2, (T + 1) * P], bf16)
        rowsum = sb("rowsum", [P, TT])
        ahead = sb("ahead", [P, TT])
        row_of = [sb(f"row_of{i}", [P, TT], i32) for i in range(2)]
        H0 = [sb(f"H0_{i}", [Q, G, D]) for i in range(2)]
        hsum = sb("hsum", [Q, G])
        hc = sb("hc", [Q, G, D])
        sq = sb("sq", [Q, G, D])
        hvar = sb("hvar", [Q, G])
        hvar_eps = sb("hvar_eps", [Q, G])
        rstd = sb("rstd", [Q, G])
        z = sb("z", [Q, G, D])
        zsplit = [sb(f"zsplit{i}", [Q, G, 2, D], fp32r) for i in range(2)]
        zT = [sb(f"zT{i}", [P, C], fp32r) for i in range(2)]
        qk = [sb(f"qk{i}", [P, C]) for i in range(2)]
        k0 = [sb(f"k0_{i}", [P, C]) for i in range(2)]
        v = [sb(f"v{i}", [Q, G, VX]) for i in range(2)]
        smax = sb("smax", [Q, G])
        nmax = [sb(f"nmax{i}", [Q, G]) for i in range(2)]
        E = [sb(f"E{i}", [Q, G, S]) for i in range(2)]
        den = [sb(f"den{i}", [Q, G]) for i in range(2)]
        ET = [sb(f"ET{i}", [Q, R * S]) for i in range(2)]
        OT = sb("OT", [P, S])
        rden = sb("rden", [Q, G])
        rden_q = sb("rden_q", [Q, G])
        rden_qk = [sb(f"rden_qk{i}", [Q, G]) for i in range(2)]
        attn = sb("attn", [Q, 2, R, D])

        usum = sb("usum", [Q, TU])
        uc = sb("uc", [Q, TU, D])
        usq = sb("usq", [Q, TU, D])
        uvar = sb("uvar", [Q, TU])
        uvar_eps = sb("uvar_eps", [Q, TU])
        urstd = sb("urstd", [Q, TU])
        uz = sb("uz", [Q, TU, D])
        usplit = sb("usplit", [Q, TU, 2, D], fp32r)
        uT = [[sb(f"uT{i}_{c}", [P, C], fp32r) for c in range(2)] for i in range(2)]
        lg_hi = sb("lg_hi", [Q, TU, NE])
        lg = sb("lg", [Q, TU, NE])
        top1 = sb("top1", [Q, TU])
        is1 = sb("is1", [Q, TU, NE])
        pr1 = sb("pr1", [Q, TU, NE])
        pm1 = sb("pm1", [Q, TU])
        sel1 = sb("sel1", [Q, TU, NE])
        lg2 = sb("lg2", [Q, TU, NE])
        top2 = sb("top2", [Q, TU])
        is2 = sb("is2", [Q, TU, NE])
        pr2 = sb("pr2", [Q, TU, NE])
        pm2 = sb("pm2", [Q, TU])
        sel2 = sb("sel2", [Q, TU, NE])
        gap = sb("gap", [Q, TU])
        tanh = sb("tanh", [Q, TU])
        wt1 = sb("wt1", [Q, TU])
        wt2 = sb("wt2", [Q, TU])
        mix1 = sb("mix1", [Q, TU, NE])
        mix2 = sb("mix2", [Q, TU, NE])
        mix = sb("mix", [Q, TU, NE])
        msplit = sb("msplit", [Q, G, 2, 2, NE], fp32r)
        mT = [sb(f"mT{i}", [P, C], fp32r) for i in range(2)]
        hid = [[sb(f"hid{i}_{c}", [HID, C]) for c in range(2)] for i in range(2)]
        mb = [sb(f"mb{i}", [P, C]) for i in range(2)]
        ye = [sb(f"ye{i}", [P, C]) for i in range(2)]
        acc = [sb(f"acc{i}", [P, C]) for i in range(2)]
        y = sb("y", [Q, PAIRS, G, D])

        PS = [ctx.enter_context(nc.psum_tensor(f"PS{i}", [P, 512], fp32)) for i in range(8)]
        srow = PS[0]
        zT_ps = PS[1][:, 0:C]
        qk_ps = PS[2][:, 0:C]
        v_ps, csum_ps = PS[3][0:Q, 0:G * VX], PS[3][:, G * VX:G * VX + TT]
        S_ps = [PS[4], PS[5]]
        ET_ps = [PS[6], PS[7]]
        OT_ps = PS[6][:, 0:S]
        back_ps = PS[7][0:Q, 0:R * P]
        hid_ps = [[PS[0], PS[1]], [PS[2], PS[3]]]
        y_ps = [PS[4], PS[5]]
        mb_ps = PS[6]
        aux_ps = PS[7]

        def uT_ps(n):
            return PS[0] if isinstance(n, int) and n == 0 else aux_ps

        def lg_ps(n, c):
            bank = PS[0] if isinstance(n, int) and n == 0 else y_ps[1 - c]
            return bank[0:Q, C:C + 2 * NE * G]

        PREP_ATTN, PREP_FFN = 4, PAIRS + 1
        wqk_ps, woT_ps = PS[4][:, 0:2 * D], PS[5][0:D, 0:D]
        wv_ps, bv_ps = PS[6][:, 0:D], PS[6][0:Q, D:2 * D]
        w1b_ps, b1_ps, b2_ps, wrb_ps = (PS[0][:, NE * i:NE * (i + 1)] for i in range(4))
        wrb_ps = wrb_ps[0:Q]

        x_cuts = [0, 1, 2, 4, 6, 8, 12, PAIRS]
        x_in = [sem(f"x_in{i}") for i in range(len(x_cuts) - 1)]
        cst_in, bo_in, attn_in, ffn_in, w1_in = sem("cst_in"), sem("bo_in"), sem("attn_in"), sem("ffn_in"), sem("w1_in")
        N_CST, N_ATTN, N_FFN, N_W1 = 2, 9, 9, 3
        pool_prep, pe_prep, act_prep, dve_prep, w1_prep = (
            sem("pool_prep"), sem("pe_prep"), sem("act_prep"), sem("dve_prep"), sem("w1_prep"))
        PRE = 5
        pre = sem("pre")
        expneg_ok, srow_ok, csum_ok = sem("expneg_ok"), sem("srow_ok"), sem("csum_ok")
        CMP, RANK = TT, 2
        cmp_ok, ranked = sem("cmp_ok"), sem("ranked")
        scattered = [sem(f"scattered{i}") for i in range(2)]
        h0_in = [sem(f"h0_in{i}") for i in range(2)]
        NRM = 4
        nrm = sem("nrm")
        hb_ok, sq_ok, rstd_ok, z_ok, zhi_ok, zlo_ok = (
            sem("hb_ok"), sem("sq_ok"), sem("rstd_ok"), sem("z_ok"), sem("zhi_ok"), sem("zlo_ok"))
        zTp_ok, zT_ok = sem("zTp_ok"), sem("zT_ok")
        qkp_ok, vp_ok, qk_ok, k0_ok, v_ok = sem("qkp_ok"), sem("vp_ok"), sem("qk_ok"), sem("k0_ok"), sem("v_ok")
        S_ok, max_ok, exp_ok = sem("S_ok"), sem("max_ok"), sem("exp_ok")
        MAX, SCL, FIN = 3, 3, 2
        scaled = sem("scaled")
        ETp_ok, ET_ok, OTp_ok, OT_ok, back_ok = (
            sem("ETp_ok"), sem("ET_ok"), sem("OTp_ok"), sem("OT_ok"), sem("back_ok"))
        h1_ok = sem("h1_ok")
        LN = 5
        ln, usq_ok, urstd_ok, uhi_ok, ulo_ok = (
            sem("ln"), sem("usq_ok"), sem("urstd_ok"), sem("uhi_ok"), sem("ulo_ok"))
        uTp_ok, uT_ok = sem("uTp_ok"), sem("uT_ok")
        lgp_ok = sem("lgp_ok")
        TOP = 23
        top, tanh_ok = sem("top"), sem("tanh_ok")
        mTp_ok, mT_ok = sem("mTp_ok"), sem("mT_ok")
        mbp_ok, mb_ok = sem("mbp_ok"), sem("mb_ok")
        hidp_ok, hid_ok, yp_ok, ye_ok, acc_ok = (
            sem("hidp_ok"), sem("hid_ok"), sem("yp_ok"), sem("ye_ok"), sem("acc_ok"))
        backB_ok, y_ok = sem("backB_ok"), sem("y_ok")
        stored = sem("stored")

        block = ctx.enter_context(nc.Block())

        def item(half, j, lag, count):
            m = half + (j - lag) // 2
            n = 2 * half + (j - lag)
            if isinstance(half, int) and not 0 <= n < count:
                return None
            return n, m, (j - lag) % 2

        A_LAG, B_LAG = 8, 3

        LAST = PAIRS + A_LAG - 1
        EARLY_B_TENSOR = {LAST - 4: [(1, [0])], LAST - 3: [(1, [1, 2])], LAST - 2: [(1, [3, 4, 5, 6, 7])]}
        EARLY_B_VECTOR = {LAST - 7: [(0, [0])], LAST - 6: [(0, [1])], LAST - 5: [(0, [2, 3, 4])],
                          LAST - 4: [(0, [5, 6, 7]), (1, [0])], LAST - 3: [(1, [1])], LAST - 2: [(1, [2])],
                          LAST - 1: [(1, [3, 4])], LAST: [(1, [5, 6, 7])]}
        EARLY_B_SCALAR = {LAST - 6: [(0, [0, 1, 2])], LAST - 5: [(0, [3, 4, 5, 6, 7])], LAST - 4: [(1, [0])],
                          LAST - 3: [(1, [1, 2])], LAST - 1: [(1, [3, 4, 5, 6, 7])]}
        EARLY_B_GPSIMD = {LAST - 6: [(0, [1])], LAST - 5: [(0, [2, 3, 4, 5, 6, 7])], LAST - 3: [(1, [0, 1])],
                          LAST - 1: [(1, [2, 3, 4, 5, 6, 7])]}

        def run(eng, step_a, step_b, early_b):
            for s in range(A_LAG):
                step_a(s // 2, s % 2)
            with eng.Fori(A_LAG // 2, PAIRS // 2) as half:
                step_a(half, 0)
                step_a(half, 1)
            for s in range(PAIRS, PAIRS + A_LAG):
                step_a(s // 2, s % 2)
                for j, experts in early_b.get(s, []):
                    step_b(0, j, experts)
            for s in range(2, B_LAG + 1):
                step_b(s // 2, s % 2)
            with eng.Fori((B_LAG + 1) // 2, UNITS // 2) as half:
                step_b(half, 0)
                step_b(half, 1)
            for s in range(UNITS, UNITS + B_LAG):
                step_b(s // 2, s % 2)

        def first(n, k=1):
            return isinstance(n, int) and n < k

        @block.sync
        def _(sp):
            def load_x(i):
                a, b = TT * x_cuts[i], TT * x_cuts[i + 1]
                sp.dma_start(X[:, a:b, :], x_tiles[:, a:b, :]).then_inc(x_in[i], 16)

            load_x(0)
            sp.dma_start(b_col[:, :], tok_b.partition_broadcast(P)).then_inc(cst_in, 16)
            load_x(1)
            sp.dma_start(bo_bc[:, :], bo.partition_broadcast(P)).then_inc(bo_in, 16)
            load_x(2)
            sp.dma_start(wo_nat[:, :], Wo).then_inc(attn_in, 16)
            sp.dma_start(bqk_col[0:D, :], bq.unsqueeze(1)).then_inc(attn_in, 16)
            sp.dma_start(bqk_col[D:P, :], bk.unsqueeze(1)).then_inc(attn_in, 16)
            sp.dma_start(bv_col[:, :], bv.unsqueeze(1)).then_inc(attn_in, 16)
            sp.dma_start(vbias[:, D:D + 1], bq[0:1].partition_broadcast(Q)).then_inc(attn_in, 16)
            sp.dma_start(vbias[:, D + 1:VX], bk[0:1].partition_broadcast(Q)).then_inc(attn_in, 16)
            load_x(3)

            def later_loads(s):
                for i in range(2):
                    rows = slice(i * D, (i + 1) * D)
                    if s == 2 + i:
                        load_x(4 + i)
                    if s == 4 + i:
                        sp.dma_start(gamma_col[rows, :], gamma.unsqueeze(1)).then_inc(ffn_in, 16)
                        sp.dma_start(wr_raw[rows, :], Wr).then_inc(ffn_in, 16)
                        sp.dma_start(b2_nat[:, i * D:(i + 1) * D], b2).then_inc(ffn_in, 16)
                    if s == 6 + i:
                        sp.dma_start(w1_raw[rows, :, :], W1.rearrange("e d h -> d e h")).then_inc(w1_in, 16)
                if s == 4:
                    load_x(6)
                if s == 6:
                    sp.dma_start(br_bc[:, :], br.partition_broadcast(Q)).then_inc(ffn_in, 16)
                    sp.dma_start(beta_col[:, :], beta.unsqueeze(1)).then_inc(ffn_in, 16)
                    sp.dma_start(b1_nat[:, :], b1).then_inc(ffn_in, 16)
                if s == 7:
                    sp.dma_start(w2_sb[:, :, :], W2.rearrange("e h d -> h e d")).then_inc(w1_in, 16)

            def step_a(half, j):
                it = item(half, j, 2, PAIRS)
                if it:
                    n, m, i = it
                    sp.wait_ge(scattered[i], 16 * TT * (m + 1))
                    sp.dma_start(H0[i][:, :, :].rearrange("p (b r) d -> p b (r d)", b=2),
                                 h_rows[:, bass.ds(2 * n, 2), :]).then_inc(h0_in[i], 16)
                if isinstance(half, int):
                    later_loads(2 * half + j)

            def step_b(half, j, experts=range(NE)):
                it = item(half, j, 3, UNITS)
                if it:
                    n, m, i = it
                    sp.wait_ge(y_ok, n + 1)
                    sp.dma_start(out_rows[:, bass.ds(4 * n, 4), :],
                                 y[:, bass.ds(2 * n, 2), :, :].rearrange("p c (b r) d -> p (c b) (r d)", r=R))\
                        .then_inc(stored, 16)

            run(sp, step_a, step_b, {})
            sp.wait_ge(stored, 16 * UNITS)

        @block.gpsimd
        def _(pool):
            pool.memset(ident[:, :], 0.0).then_inc(pool_prep, 1)
            pool.memset(later[:, :], 1.0).then_inc(pool_prep, 1)
            pool.memset(ones_bf[:, :], 1.0).then_inc(pool_prep, 1)
            pool.memset(neg_half[:, :], -0.5).then_inc(pool_prep, 1)
            pool.wait_ge(pool_prep, 4)
            pool.affine_select(out=ident[:, :], in_=ident[:, :], compare_op=ALU.not_equal, fill=1.0,
                               base=0, pattern=[[-1, P]], channel_multiplier=1).then_inc(pool_prep, 1)
            pool.affine_select(out=later[:, :], in_=later[:, :], compare_op=ALU.is_gt, fill=0.0,
                               base=0, pattern=[[1, T * P]], channel_multiplier=-1).then_inc(pool_prep, 1)
            pool.iota(row_index[:, :], pattern=[[N, B], [P, T]], base=0, channel_multiplier=1,
                      allow_small_or_imprecise_dtypes=True).then_inc(pool_prep, 1)
            pool.iota(falling[:, :], pattern=[[-1, NE]], base=NE, channel_multiplier=0,
                      allow_small_or_imprecise_dtypes=True).then_inc(pool_prep, 1)
            for i in range(2):
                pool.memset(k0[i][:, :], 0.0).then_inc(pool_prep, 1)
                pool.memset(mT[i][:, :].bitcast(fp32), 0.0).then_inc(pool_prep, 1)
            pool.memset(pick[:, :, :, :], 0.0).then_inc(pool_prep, 1)
            pool.wait_ge(pool_prep, POOL_PREP - 2)
            for part in range(2):
                pool.affine_select(out=pick[:, :, :, :], in_=pick[:, :, :, :], compare_op=ALU.not_equal,
                                   fill=1.0, base=-2 * NE * part, pattern=[[-1, NE], [-NE, 2], [0, D]],
                                   channel_multiplier=1).then_inc(pool_prep, 1)
                pool.wait_ge(pool_prep, POOL_PREP - 1 + part)

            pool.wait_ge(bo_in, 16)

            def prepare(s):
                if s == PREP_FFN + 5:
                    pool.wait_ge(act_prep, 8)
                    pool.tensor_tensor(w1_lo[:, :, :], w1_g[:, :, :], w1_hi[:, :, :], ALU.subtract)\
                        .then_inc(w1_prep, 1)

            def step_a(half, j):
                send = item(half, j, 1, PAIRS)
                it = item(half, j, 3, PAIRS)
                if it:
                    n, m, i = it
                    pool.wait_ge(h0_in[i], 16 * (m + 1))
                    pool.wait_ge(pool_prep, POOL_PREP)
                    pool.tensor_tensor(H1[:, bass.ds(n, 1), :].rearrange("p a (g d) -> p (a g) d", d=D),
                                       H0[i][:, :, :], bo_bc[0:Q, None, :].to_broadcast([Q, G, D]), ALU.add)\
                        .then_inc(hb_ok, 1)
                it = item(half, j, 4, PAIRS)
                if send:
                    pool.wait_ge(pre, PRE * (send[0] + 1))
                    pool.wait_ge(ranked, RANK * (send[0] + 1))
                    if not first(send[0], 2):
                        pool.wait_ge(hb_ok, send[0] - 1)
                        pool.wait_ge(nrm, NRM * (send[0] - 2) + 2)
                if it:
                    n, m, i = it
                    pool.wait_ge(zhi_ok, n + 1)
                    pool.tensor_tensor(zsplit[i][:, :, 1, :], z[:, :, :], zsplit[i][:, :, 0, :], ALU.subtract)\
                        .then_inc(zlo_ok, 1)

                def scatter(tiles):
                    i = send[2]
                    for t in tiles:
                        pool.indirect_dma_start(
                            out=h_sorted[:, :],
                            out_offset=bass.IndirectOffsetOnAxis(ap=row_of[i][:, t:t + 1], axis=0),
                            in_=h[i][:, t, :], in_offset=None).then_inc(scattered[i], 16)

                if send:
                    scatter(range(1))
                it = item(half, j, 3, PAIRS)
                if it:
                    n, m, i = it
                    if not first(n):
                        pool.wait_ge(z_ok, n)
                    pool.wait_ge(nrm, NRM * (n + 1))
                    pool.tensor_tensor(rstd[:, :], hvar_eps[:, :], neg_half[:, 0:G], ALU.pow).then_inc(rstd_ok, 1)
                if send:
                    scatter(range(1, TT))
                if isinstance(half, int):
                    prepare(2 * half + j)

            def step_b(half, j, experts=range(NE)):
                nxt, main = item(half, j, 0, UNITS), item(half, j, 2, UNITS)
                for e in experts:
                    if main and e >= 1:
                        n, m, i = main
                        pool.wait_ge(ye_ok, NE * n + e + 1)
                        if e > 1:
                            pool.wait_ge(acc_ok, (NE - 1) * n + e - 1)
                        pool.tensor_tensor(acc[i][:, :], acc[i][:, :], ye[e % 2][:, :], ALU.add)\
                            .then_inc(acc_ok, 1)
                    if nxt and e == 1:
                        n, m, i = nxt
                        pool.wait_ge(ln, LN * n + 4)
                        pool.tensor_tensor(urstd[:, :], uvar_eps[:, :], neg_half[:, :], ALU.pow)\
                            .then_inc(urstd_ok, 1)
                    if nxt and e == 5:
                        n, m, i = nxt
                        pool.wait_ge(uhi_ok, n + 1)
                        pool.tensor_tensor(usplit[:, :, 1, :], uz[:, :, :], usplit[:, :, 0, :], ALU.subtract)\
                            .then_inc(ulo_ok, 1)

            run(pool, step_a, step_b, EARLY_B_GPSIMD)

        @block.scalar
        def _(act):
            act.dma_start(w_bc[:, :], tok_w.partition_broadcast(P)).then_inc(cst_in, 16)
            act.dma_start(wqk_nat[:, 0:2, :], Wq.unsqueeze(1).to_broadcast([D, 2, D])).then_inc(attn_in, 16)
            act.dma_start(wqk_nat[:, 2:4, :], Wk.unsqueeze(1).to_broadcast([D, 2, D])).then_inc(attn_in, 16)
            act.dma_start(wv_nat[:, :, :], Wv.unsqueeze(1).to_broadcast([D, 2, D])).then_inc(attn_in, 16)

            def prepare(s):
                if s == PREP_ATTN:
                    act.wait_ge(pe_prep, 1)
                    act.activation(wqk_hi[:, :], wqk_ps, ACT.Copy).then_inc(act_prep, 1)
                    act.activation(woT[:, :], woT_ps, ACT.Copy).then_inc(act_prep, 1)
                    act.wait_ge(pe_prep, 2)
                    act.activation(wvx_hi[:, 0:D], wv_ps, ACT.Copy).then_inc(act_prep, 1)
                    act.activation(wvx_hi[:, D:VX], wqk_ps[:, 0:D + 1:D], ACT.Copy).then_inc(act_prep, 1)
                    act.activation(vbias[:, 0:D], bv_ps, ACT.Copy).then_inc(act_prep, 1)
                if s == PREP_FFN + 1:
                    act.wait_ge(dve_prep, 4)
                    act.activation(wr_split[:, 0, :], wr_g[:, :], ACT.Copy).then_inc(act_prep, 1)
                if s == PREP_FFN + 2:
                    act.wait_ge(w1_in, 16 * N_W1)
                    act.activation(w1_g[:, :, :], w1_raw[:, :, :], ACT.Identity, scale=gamma_col[:, 0:1])\
                        .then_inc(act_prep, 1)
                if s == PREP_FFN + 4:
                    act.wait_ge(act_prep, 7)
                    act.activation(w1_hi[:, :, :], w1_g[:, :, :], ACT.Copy).then_inc(act_prep, 1)
                    act.wait_ge(pool_prep, POOL_PREP)
                    act.activation(spread[:, :, :], pick[:, :, :, :].rearrange("p e c d -> p e (c d)"), ACT.Copy)\
                        .then_inc(act_prep, 1)

            def step_a(half, j):
                if isinstance(half, int):
                    prepare(2 * half + j)
                it = item(half, j, 5, PAIRS)
                if it:
                    n, m, i = it
                    act.wait_ge(zTp_ok, n + 1)
                    if not first(n, 2):
                        act.wait_ge(vp_ok, n - 1)
                    act.activation(zT[i][:, :], zT_ps, ACT.Copy).then_inc(zT_ok, 1)
                turned = item(half, j, 7, PAIRS)

                def copy_ET(b):
                    n, m, i = turned
                    act.wait_ge(ETp_ok, 2 * n + b + 1)
                    if not first(n):
                        act.wait_ge(OTp_ok, n)
                    act.activation(ET[b][:, :], ET_ps[b][0:Q, 0:R * S], ACT.Copy).then_inc(ET_ok, 1)

                if turned:
                    copy_ET(0)
                    copy_ET(1)
                it = item(half, j, 4, PAIRS)
                if it:
                    n, m, i = it
                    act.wait_ge(z_ok, n + 1)
                    if not first(n, 2):
                        act.wait_ge(zTp_ok, n - 1)
                        act.wait_ge(zlo_ok, n - 1)
                    act.activation(zsplit[i][:, :, 0, :], z[:, :, :], ACT.Copy).then_inc(zhi_ok, 1)
                it = item(half, j, 5, PAIRS)
                if it:
                    n, m, i = it
                    act.wait_ge(qkp_ok, n + 1)
                    if not first(n, 2):
                        act.wait_ge(S_ok, 2 * (n - 1))
                    act.activation(qk[i][:, :], qk_ps, ACT.Identity, bias=bqk_col[:, 0:1]).then_inc(qk_ok, 1)
                    act.activation(k0[i][0:D, :], qk_ps[D:P, :], ACT.Identity, bias=bqk_col[D:P, 0:1])\
                        .then_inc(k0_ok, 1)
                it = item(half, j, 3, PAIRS)
                if it:
                    n, m, i = it
                    act.wait_ge(nrm, NRM * n + 2)
                    act.activation(sq[:, :, :], hc[:, :, :], ACT.Square, scale=D ** -0.5).then_inc(sq_ok, 1)
                it = item(half, j, 7, PAIRS)
                if it:
                    n, m, i = it
                    act.wait_ge(OTp_ok, n + 1)
                    if not first(n):
                        act.wait_ge(back_ok, n)
                    act.activation(OT[:, :], OT_ps, ACT.Copy).then_inc(OT_ok, 1)
                it = item(half, j, 0, PAIRS)
                if it:
                    n, m, i = it
                    act.wait_ge(pre, PRE * n + 2)
                    act.activation(expneg[:, :], score[i][:, :], ACT.Exp, scale=-1.0).then_inc(expneg_ok, 1)
                soft = item(half, j, 6, PAIRS)

                def softmax(b):
                    i = soft[2]
                    for g in range(R * b, R * (b + 1)):
                        last = act.activation(E[i][:, g, :], S_ps[b][0:Q, (g % R) * S:(g % R + 1) * S],
                                              ACT.Exp, bias=nmax[i][:, g:g + 1], scale=SCALE,
                                              accum_out=den[i][:, g:g + 1])
                    return last

                if soft:
                    n, m, i = soft
                    act.wait_ge(max_ok, MAX * (n + 1))
                    if not first(n, 2):
                        act.wait_ge(ETp_ok, 2 * (n - 1))
                        act.wait_ge(scaled, SCL * (n - 1))
                    softmax(0)
                    softmax(1).then_inc(exp_ok, 1)

            def mix_out(it, e):
                n, m, i = it
                k = NE * n + e
                act.wait_ge(mbp_ok, k + 1)
                if not first(n) or e >= 2:
                    act.wait_ge(ye_ok, k - 1)
                act.activation(mb[e % 2][:, :], mb_ps[:, 0:C], ACT.Copy).then_inc(mb_ok, 1)

            def step_b(half, j, experts=range(NE)):
                nxt, prep, main, prev = (item(half, j, lag, UNITS) for lag in range(4))
                for e in experts:
                    if main and e >= 1:
                        mix_out(main, e - 1)
                    if prev and e == 0:
                        mix_out(prev, NE - 1)
                    if nxt and e == 2:
                        n, m, i = nxt
                        act.wait_ge(ln, LN * n + 2)
                        act.activation(usq[:, :, :], uc[:, :, :], ACT.Square, scale=((1.0 + EPS) / D) ** 0.5)\
                            .then_inc(usq_ok, 1)
                    if main:
                        n, m, i = main
                        k = NE * n + e
                        for c in range(2):
                            act.wait_ge(hidp_ok, 2 * k + c + 1)
                            if not first(n) or e >= 2:
                                act.wait_ge(yp_ok, k - 1)
                            act.activation(hid[e % 2][c][:, :], hid_ps[e % 2][c][:, 0:C], ACT.Gelu,
                                           bias=b1_eff[:, e:e + 1]).then_inc(hid_ok, 1)
                    if main and e == 0:
                        n, m, i = main
                        act.wait_ge(mTp_ok, n + 1)
                        act.activation(mT[i][0:4 * NE, :], mb_ps[0:4 * NE, 0:C], ACT.Copy).then_inc(mT_ok, 1)
                    if prep and e < 2:
                        n, m, i = prep
                        act.wait_ge(uTp_ok, 2 * n + e + 1)
                        act.activation(uT[i][e][:, :], uT_ps(n)[:, 0:C], ACT.Copy).then_inc(uT_ok, 1)
                    if prep and e == 5:
                        n, m, i = prep
                        act.wait_ge(top, TOP * n + 15)
                        act.activation(tanh[:, :], gap[:, :], ACT.Tanh, scale=0.5).then_inc(tanh_ok, 1)
                    if nxt and e == 6:
                        n, m, i = nxt
                        act.wait_ge(ln, LN * (n + 1))
                        if not first(n):
                            act.wait_ge(uTp_ok, 2 * n)
                        act.activation(usplit[:, :, 0, :], uz[:, :, :], ACT.Copy).then_inc(uhi_ok, 1)

            run(act, step_a, step_b, EARLY_B_SCALAR)

        @block.tensor
        def _(pe):
            def prepare(s):
                if s == PREP_ATTN:
                    pe.wait_ge(attn_in, 16 * N_ATTN)
                    pe.transpose(wqk_ps[:, 0:D], wqk_nat[:, 0:2, :].rearrange("o c d -> o (c d)"), ident[0:D, 0:D])
                    pe.transpose(wqk_ps[:, D:2 * D], wqk_nat[:, 2:4, :].rearrange("o c d -> o (c d)"), ident[0:D, 0:D])
                    pe.transpose(woT_ps, wo_nat[:, :], ident[0:D, 0:D]).then_inc(pe_prep, 1)
                    pe.wait_ge(act_prep, 2)
                    pe.matmul(wv_ps, wv_nat[:, :, :].rearrange("o c d -> o (c d)"), woT[:, :], start=True, stop=True)
                    pe.matmul(bv_ps, bv_col[:, 0:1].to_broadcast([D, Q]), woT[:, :],
                              start=True, stop=True).then_inc(pe_prep, 1)
                if s == PREP_FFN:
                    pe.wait_ge(ffn_in, 16 * N_FFN)
                    pe.wait_ge(w1_in, 16 * N_W1)
                    for e in range(NE):
                        pe.matmul(w1b_ps[:, e:e + 1], w1_raw[0:D, e, :], beta_col[:, :], start=True, stop=True)
                    pe.matmul(wrb_ps, beta_col[:, 0:1].to_broadcast([D, Q]), wr_raw[0:D, :], start=True, stop=True)
                    pe.transpose(b1_ps, b1_nat[:, :], ident[0:NE, 0:NE])
                    pe.transpose(b2_ps, b2_nat[:, :], ident[0:NE, 0:NE]).then_inc(pe_prep, 1)
                if s == 5:
                    pe.wait_ge(act_prep, 5)
                    pe.wait_ge(dve_prep, 3)

            pe.wait_ge(pool_prep, 5)

            def step_a(half, j):
                if isinstance(half, int):
                    prepare(2 * half + j)
                beats, project, before = (item(half, j, lag, PAIRS) for lag in (1, 5, 6))
                if project:
                    n, m, i = project
                    pe.wait_ge(zlo_ok, n + 1)
                    if not first(n):
                        pe.wait_ge(zT_ok, n)
                    for g in range(G):
                        last = pe.transpose(zT_ps[:, g * Q:(g + 1) * Q],
                                            zsplit[i][:, g, :, :].rearrange("p c d -> p (c d)").bitcast(fp32),
                                            ident[0:Q, 0:Q])
                    last.then_inc(zTp_ok, 1)
                last_scores = item(half, j, 7, PAIRS)

                def transpose_exp(b):
                    n, m, i = last_scores
                    if b == 0:
                        pe.wait_ge(exp_ok, n + 1)
                        if not first(n):
                            pe.wait_ge(OT_ok, n)
                    elif not first(n):
                        pe.wait_ge(h1_ok, FIN * (n - 1) + 1)
                    for kt in range(R):
                        for qt in range(R):
                            last = pe.transpose(ET_ps[b][0:Q, kt * S + qt * Q:kt * S + (qt + 1) * Q],
                                                E[i][:, R * b + qt, kt * Q:(kt + 1) * Q], ident[0:Q, 0:Q])
                    last.then_inc(ETp_ok, 1)

                if last_scores:
                    transpose_exp(0)
                if before:
                    n, m, i = before
                    pe.wait_ge(qk_ok, n + 1)
                    pe.wait_ge(k0_ok, n + 1)
                    if not first(n):
                        pe.wait_ge(exp_ok, n)
                    for b in range(2):
                        for qt in range(R):
                            c0 = b * S + qt * Q
                            last = pe.matmul(S_ps[b][0:Q, qt * S:(qt + 1) * S], qk[i][:, c0:c0 + Q],
                                             k0[i][:, b * S:(b + 1) * S], start=True, stop=True)
                        last.then_inc(S_ok, 1)
                if last_scores:
                    transpose_exp(1)
                if project:
                    n, m, i = project
                    pe.wait_ge(zT_ok, n + 1)
                    if not first(n):
                        pe.wait_ge(k0_ok, n)
                    pe.matmul(qk_ps, wqk_hi[:, :], zT[i][:, :], start=True, stop=False)
                    pe.matmul(qk_ps, wqk_lo[:, :], zT[i][:, :], start=False, stop=True).then_inc(qkp_ok, 1)
                if beats:
                    n, m, i = beats
                    pe.wait_ge(cmp_ok, CMP * (n + 1))
                    if before:
                        pe.wait_ge(v_ok, before[0] + 1)
                    for b in range(2):
                        for t in range(T):
                            col = csum_ps[:, T * b + t:T * b + t + 1]
                            for a in range(t + 1):
                                c0 = a * T * P + (t - a) * P
                                last = pe.matmul(col, greater[:, b, c0:c0 + P], ones_bf[:, :],
                                                 start=(a == 0), stop=(a == t))
                    last.then_inc(csum_ok, 1)
                it = item(half, j, 7, PAIRS)
                if it:
                    n, m, i = it
                    pe.wait_ge(v_ok, n + 1)
                    for b in range(2):
                        pe.wait_ge(ET_ok, 2 * n + b + 1)
                        for kt in range(R):
                            last = pe.matmul(OT_ps[b * D:(b + 1) * D, :], v[i][:, R * b + kt, 0:D],
                                             ET[b][:, kt * S:(kt + 1) * S], start=(kt == 0), stop=(kt == R - 1))
                    last.then_inc(OTp_ok, 1)
                if project:
                    n, m, i = project
                    if not first(n):
                        pe.wait_ge(v_ok, n)
                    if beats:
                        pe.wait_ge(ranked, RANK * beats[0] + 1)
                    for g in range(G):
                        for w in (wvx_hi, wvx_lo):
                            last = pe.matmul(v_ps[:, g * VX:(g + 1) * VX], zT[i][:, g * Q:(g + 1) * Q], w[:, :],
                                             start=(w is wvx_hi), stop=(w is wvx_lo))
                    last.then_inc(vp_ok, 1)
                it = item(half, j, 0, PAIRS)
                if it:
                    n, m, i = it
                    pe.wait_ge(pre, PRE * n + 2)
                    if not first(n):
                        pe.wait_ge(cmp_ok, CMP * n)
                    for t in range(TT):
                        last = pe.transpose(srow[:, t * P:(t + 1) * P],
                                            score[i][:, t:t + 1].to_broadcast([P, P]), ident[:, :])
                    last.then_inc(srow_ok, 1)
                it = item(half, j, 7, PAIRS)
                if it:
                    n, m, i = it
                    pe.wait_ge(OT_ok, n + 1)
                    pe.wait_ge(ET_ok, 2 * (n + 1))
                    for r in range(R):
                        last = pe.transpose(back_ps[:, r * P:(r + 1) * P], OT[:, r * Q:(r + 1) * Q], ident[:, :])
                    last.then_inc(back_ok, 1)

            def step_b(half, j, experts=range(NE)):
                if isinstance(half, int) and (half, j) == (0, 1) and 0 in experts:
                    pe.wait_ge(dve_prep, DVE_PREP)
                if isinstance(half, int) and (half, j) == (1, 0):
                    pe.wait_ge(act_prep, ACT_PREP)
                    pe.wait_ge(w1_prep, 1)
                    pe.wait_ge(top, 4)
                prep, main, prev = (item(half, j, lag, UNITS) for lag in range(1, 4))
                for e in experts:
                    late, f = (main, e - 1) if e else (prev, NE - 1)
                    if late:
                        n, m, i = late
                        k = NE * n + f
                        if f == 0:
                            pe.wait_ge(mT_ok, n + 1)
                        if not first(n) or f:
                            pe.wait_ge(mb_ok, k)
                        pe.matmul(mb_ps[:, 0:C], spread[:, f, :], mT[i][:, :], start=True, stop=True)\
                            .then_inc(mbp_ok, 1)
                    if main:
                        n, m, i = main
                        k = NE * n + e
                        if not first(n) or e >= 2:
                            pe.wait_ge(hid_ok, 2 * (k - 1))
                        for w in (w1_hi, w1_lo):
                            for c in range(2):
                                last = pe.matmul(hid_ps[e % 2][c][:, 0:C], w[:, e, :], uT[i][c][:, :],
                                                 start=(w is w1_hi), stop=(w is w1_lo))
                                if w is w1_lo:
                                    last.then_inc(hidp_ok, 1)
                    if prep and 2 <= e < 4:
                        n, m, i = prep
                        c = e - 2
                        if main:
                            pe.wait_ge(uT_ok, 2 * n + c + 1)
                            if not first(main[0]) or f >= 2:
                                pe.wait_ge(ye_ok, NE * main[0] + f - 1)
                        else:
                            pe.wait_ge(uT_ok, 2)
                            if c == 1:
                                pe.wait_ge(top, 2)
                        for g in range(G):
                            last = pe.matmul(lg_ps(n, c)[:, 2 * NE * g:2 * NE * (g + 1)],
                                             uT[i][c][:, g * Q:(g + 1) * Q],
                                             wr_split[:, :, :].rearrange("p a e -> p (a e)"), start=True, stop=True)
                        last.then_inc(lgp_ok, 1)
                    if late:
                        n, m, i = late
                        k = NE * n + f
                        if not first(n) or f >= 2:
                            pe.wait_ge(ye_ok, k - 1)
                        if prep and 4 <= e < 6:
                            pe.wait_ge(top, TOP * prep[0] + 2 * (e - 3))
                        for c in range(2):
                            pe.wait_ge(hid_ok, 2 * k + c + 1)
                            last = pe.matmul(y_ps[f % 2][c * D:(c + 1) * D, 0:C], w2_sb[:, f, :],
                                             hid[f % 2][c][:, :], start=True, stop=True)
                        last.then_inc(yp_ok, 1)
                    if main and e == 0:
                        n, m, i = main
                        pe.wait_ge(top, TOP * (n + 1))
                        if not first(n):
                            pe.wait_ge(mb_ok, NE * n)
                        else:
                            pe.wait_ge(h1_ok, FIN * PAIRS - 1)
                        for g in range(G):
                            last = pe.transpose(
                                mb_ps[0:4 * NE, g * Q:(g + 1) * Q],
                                msplit[:, g, :, :, :].rearrange("p a c e -> p (a c e)").bitcast(fp32),
                                ident[0:Q, 0:Q])
                        last.then_inc(mTp_ok, 1)
                    if prep and e < 2:
                        n, m, i = prep
                        if e == 0:
                            pe.wait_ge(ulo_ok, n + 1)
                            if not first(n, 3):
                                pe.wait_ge(y_ok, n - 2)
                        else:
                            pe.wait_ge(uT_ok, 2 * n + 1)
                        for g in range(G):
                            last = pe.transpose(uT_ps(n)[:, g * Q:(g + 1) * Q],
                                                usplit[:, G * e + g, :, :].rearrange("p c d -> p (c d)").bitcast(fp32),
                                                ident[0:Q, 0:Q])
                        last.then_inc(uTp_ok, 1)
                    if prev and e == 4:
                        n, m, i = prev
                        pe.wait_ge(acc_ok, (NE - 1) * (n + 1))
                        if prep:
                            pe.wait_ge(uT_ok, 2 * (prep[0] + 1))
                        for g in range(G):
                            last = pe.transpose(aux_ps[0:Q, g * P:(g + 1) * P], acc[i][:, g * Q:(g + 1) * Q],
                                                ident[:, :])
                        last.then_inc(backB_ok, 1)

            run(pe, step_a, step_b, EARLY_B_TENSOR)

        @block.vector
        def _(dve):
            def prepare(s):
                if s == 1:
                    dve.wait_ge(pool_prep, POOL_PREP)
                if s == PREP_ATTN:
                    dve.wait_ge(act_prep, 5)
                    dve.tensor_tensor(wqk_lo[:, :], wqk_ps, wqk_hi[:, :], ALU.subtract).then_inc(dve_prep, 1)
                    dve.tensor_tensor(wvx_lo[:, 0:D], wv_ps, wvx_hi[:, 0:D], ALU.subtract).then_inc(dve_prep, 1)
                    dve.tensor_tensor(wvx_lo[:, D:VX], wqk_ps[:, 0:D + 1:D], wvx_hi[:, D:VX], ALU.subtract)\
                        .then_inc(dve_prep, 1)
                if s == PREP_FFN:
                    dve.wait_ge(ffn_in, 16 * N_FFN)
                    dve.tensor_scalar(wr_g[:, :], wr_raw[:, :], gamma_col[:, 0:1], None, ALU.mult).then_inc(dve_prep, 1)
                if s == PREP_FFN + 1:
                    dve.wait_ge(pe_prep, 3)
                    dve.tensor_copy(b1_T[:, :], b1_ps).then_inc(dve_prep, 1)
                    dve.tensor_copy(b2_col[:, :], b2_ps).then_inc(dve_prep, 1)
                    dve.wait_ge(dve_prep, 5)
                    dve.tensor_tensor(b1_eff[:, :], w1b_ps, b1_T[:, :], ALU.add).then_inc(dve_prep, 1)
                    dve.tensor_tensor(br_eff[:, :], wrb_ps, br_bc[:, :], ALU.add).then_inc(dve_prep, 1)
                if s == PREP_FFN + 2:
                    dve.wait_ge(act_prep, 6)
                    dve.tensor_tensor(wr_split[:, 1, :], wr_g[:, :], wr_split[:, 0, :], ALU.subtract)\
                        .then_inc(dve_prep, 1)

            dve.wait_ge(cst_in, 16 * N_CST)

            def score_sums(n, m, i):
                if isinstance(n, int):
                    for a in x_cuts[:-1]:
                        if a == n or (n == A_LAG - 1 and a > n):
                            dve.wait_ge(x_in[x_cuts.index(a)], 16)
                for t in range(TT):
                    last = dve.scalar_tensor_tensor(
                        out=xw[:, t, :], in0=X[:, bass.ds(TT * n + t, 1), :].rearrange("p a d -> p (a d)"), scalar=1.0,
                        in1=w_bc[:, :], op0=ALU.mult, op1=ALU.mult, accum_out=ssum[:, t:t + 1])
                last.then_inc(pre, 1)

            def score_bias(n, m, i):
                dve.wait_ge(pre, PRE * n + 1)
                dve.tensor_scalar(score[i][:, :], ssum[:, :], b_col[:, 0:1], None, ALU.add).then_inc(pre, 1)

            def gate_one_plus(n, m, i):
                dve.wait_ge(expneg_ok, n + 1)
                dve.tensor_scalar(gate1[:, :], expneg[:, :], 1.0, None, ALU.add).then_inc(pre, 1)

            def gate_value(n, m, i):
                dve.wait_ge(pre, PRE * n + 3)
                dve.reciprocal(gate[:, :], gate1[:, :]).then_inc(pre, 1)

            def gated(n, m, i):
                dve.wait_ge(pre, PRE * n + 4)
                if not first(n, 2):
                    dve.wait_ge(scattered[i], 16 * TT * m)
                dve.tensor_tensor(h[i][:, :, :], X[:, bass.ds(TT * n, TT), :],
                                  gate[:, :, None].to_broadcast([P, TT, D]), ALU.mult).then_inc(pre, 1)

            def compare(n, m, i):
                dve.wait_ge(srow_ok, n + 1)
                if not first(n):
                    dve.wait_ge(csum_ok, n)
                    dve.wait_ge(ranked, RANK * n)
                for b in range(2):
                    for t in range(T):
                        c0, w = t * T * P, (T - t) * P
                        g = T * b + t
                        dve.scalar_tensor_tensor(
                            out=greater[:, b, c0:c0 + w], in0=srow[:, (g * P):(T * b + T) * P],
                            scalar=score[i][:, g:g + 1], in1=later[:, 0:w], op0=ALU.is_gt, op1=ALU.mult,
                            accum_out=rowsum[:, g:g + 1]).then_inc(cmp_ok, 1)

            def rank_less_index(n, m, i):
                dve.wait_ge(csum_ok, n + 1)
                dve.wait_ge(cmp_ok, CMP * (n + 1))
                dve.tensor_tensor(ahead[:, :], rowsum[:, :], csum_ps, ALU.subtract).then_inc(ranked, 1)

            def rank_row(n, m, i):
                dve.wait_ge(ranked, RANK * n + 1)
                if not first(n, 2):
                    dve.wait_ge(scattered[i], 16 * TT * m)
                dve.tensor_tensor(row_of[i][:, :], ahead[:, :], row_index[:, bass.ds(TT * n, TT)], ALU.add)\
                    .then_inc(ranked, 1)

            def norm_sum(n, m, i):
                dve.wait_ge(h0_in[i], 16 * (m + 1))
                dve.tensor_reduce(hsum[:, :], H0[i][:, :, :], AX.X, ALU.add).then_inc(nrm, 1)

            def norm_center(n, m, i):
                dve.wait_ge(nrm, NRM * n + 1)
                dve.scalar_tensor_tensor(out=hc[:, :, :], in0=hsum[:, :, None].to_broadcast([Q, G, D]),
                                         scalar=1.0 / D, in1=H0[i][:, :, :], op0=ALU.mult, op1=ALU.subtract)\
                    .then_inc(nrm, 1)

            def norm_var(n, m, i):
                dve.wait_ge(sq_ok, n + 1)
                dve.tensor_reduce(hvar[:, :], sq[:, :, :], AX.X, ALU.add).then_inc(nrm, 1)

            def norm_var_eps(n, m, i):
                dve.wait_ge(nrm, NRM * n + 3)
                dve.tensor_scalar(hvar_eps[:, :], hvar[:, :], EPS, None, ALU.add).then_inc(nrm, 1)

            def norm_z(n, m, i):
                dve.wait_ge(rstd_ok, n + 1)
                if not first(n):
                    dve.wait_ge(zlo_ok, n)
                dve.scalar_tensor_tensor(out=z[:, :, :], in0=hc[:, :, :], scalar=-1.0,
                                         in1=rstd[:, :, None].to_broadcast([Q, G, D]), op0=ALU.mult, op1=ALU.mult)\
                    .then_inc(z_ok, 1)

            def values(n, m, i):
                dve.wait_ge(vp_ok, n + 1)
                if not first(n, 2):
                    dve.wait_ge(OTp_ok, n - 1)
                    dve.wait_ge(scaled, SCL * (n - 1))
                dve.tensor_tensor(v[i][:, :, :], v_ps.rearrange("p (g c) -> p g c", g=G),
                                  vbias[:, None, :].to_broadcast([Q, G, VX]), ALU.add).then_inc(v_ok, 1)

            def row_max(n, m, i, b):
                dve.wait_ge(S_ok, 2 * n + b + 1)
                dve.tensor_reduce(smax[:, R * b:R * (b + 1)],
                                  S_ps[b][0:Q, 0:R * S].rearrange("p (r s) -> p r s", r=R), AX.X, ALU.max)\
                    .then_inc(max_ok, 1)

            def row_max_0(n, m, i):
                row_max(n, m, i, 0)

            def row_max_1(n, m, i):
                row_max(n, m, i, 1)

            def minus_max(n, m, i):
                dve.wait_ge(max_ok, MAX * n + 2)
                if not first(n, 2):
                    dve.wait_ge(exp_ok, n - 1)
                dve.tensor_scalar(nmax[i][:, :], smax[:, :], -SCALE, None, ALU.mult).then_inc(max_ok, 1)

            def one_over_den(n, m, i):
                dve.wait_ge(exp_ok, n + 1)
                dve.reciprocal(rden[:, :], den[i][:, :]).then_inc(scaled, 1)

            def mask_q(n, m, i):
                dve.wait_ge(scaled, SCL * n + 1)
                dve.wait_ge(v_ok, n + 1)
                dve.scalar_tensor_tensor(out=rden_q[:, :], in0=v[i][:, :, D], scalar=0.0, in1=rden[:, :],
                                         op0=ALU.not_equal, op1=ALU.mult).then_inc(scaled, 1)

            def mask_k(n, m, i):
                dve.wait_ge(scaled, SCL * n + 2)
                dve.scalar_tensor_tensor(out=rden_qk[i][:, :], in0=v[i][:, :, D + 1], scalar=0.0, in1=rden_q[:, :],
                                         op0=ALU.not_equal, op1=ALU.mult).then_inc(scaled, 1)

            def attention(n, m, i):
                dve.wait_ge(scaled, SCL * (n + 1))
                dve.wait_ge(back_ok, n + 1)
                for b in range(2):
                    last = dve.tensor_tensor(
                        attn[:, b, :, :], back_ps.rearrange("p (r b d) -> p b r d", r=R, b=2)[:, b, :, :],
                        rden_qk[i][:, R * b:R * (b + 1), None].to_broadcast([Q, R, D]), ALU.mult)
                last.then_inc(h1_ok, 1)

            def residual(n, m, i):
                dve.wait_ge(hb_ok, n + 1)
                dve.wait_ge(h1_ok, FIN * n + 1)
                H1n = H1[:, bass.ds(n, 1), :].rearrange("p a f -> p (a f)")
                dve.tensor_tensor(H1n, attn[:, :, :, :].rearrange("p b r d -> p (b r d)"), H1n, ALU.add)\
                    .then_inc(h1_ok, 1)

            def step_a(half, j):
                if isinstance(half, int):
                    prepare(2 * half + j)
                for stage, lag in (
                        (attention, 8), (score_sums, 0), (norm_z, 4), (compare, 1), (score_bias, 0), 
                        (norm_sum, 3), (row_max_0, 6), (norm_center, 3), (rank_less_index, 1), (row_max_1, 6),
                        (rank_row, 1), (minus_max, 6), (norm_var, 3), (one_over_den, 7), (residual, 8),
                        (mask_q, 7), (norm_var_eps, 3), (gate_one_plus, 0), (mask_k, 7), (gate_value, 0),
                        (values, 5), (gated, 0)):
                    it = item(half, j, lag, PAIRS)
                    if it:
                        stage(*it)

            def norm(it, part):
                n, m, i = it
                rows = H1[:, bass.ds(2 * n, 2), :].rearrange("p c (g d) -> p (c g) d", d=D)
                if part == 0:
                    dve.tensor_reduce(usum[:, :], rows, AX.X, ALU.add).then_inc(ln, 1)
                    dve.wait_ge(ln, LN * n + 1)
                    dve.scalar_tensor_tensor(out=uc[:, :, :], in0=usum[:, :, None].to_broadcast([Q, TU, D]),
                                             scalar=1.0 / D, in1=rows, op0=ALU.mult, op1=ALU.subtract)\
                        .then_inc(ln, 1)
                if part == 1:
                    dve.wait_ge(usq_ok, n + 1)
                    dve.tensor_reduce(uvar[:, :], usq[:, :, :], AX.X, ALU.add).then_inc(ln, 1)
                    dve.wait_ge(ln, LN * n + 3)
                    dve.tensor_scalar(uvar_eps[:, :], uvar[:, :], EPS * EPS, None, ALU.add).then_inc(ln, 1)
                if part == 2:
                    dve.wait_ge(urstd_ok, n + 1)
                    if not first(n):
                        dve.wait_ge(ulo_ok, n)
                    dve.scalar_tensor_tensor(out=uz[:, :, :], in0=uc[:, :, :], scalar=-1.0,
                                             in1=urstd[:, :, None].to_broadcast([Q, TU, D]),
                                             op0=ALU.mult, op1=ALU.mult).then_inc(ln, 1)

            def largest(done, src, top_, is_, pr_, pm_):
                dve.tensor_reduce(top_[:, :], src[:, :, :], AX.X, ALU.max).then_inc(top, 1)
                dve.wait_ge(top, done + 1)
                dve.tensor_tensor(is_[:, :, :], src[:, :, :], top_[:, :, None].to_broadcast([Q, TU, NE]),
                                  ALU.is_equal).then_inc(top, 1)
                dve.wait_ge(top, done + 2)
                dve.tensor_tensor(pr_[:, :, :], is_[:, :, :], falling[:, None, :].to_broadcast([Q, TU, NE]),
                                  ALU.mult).then_inc(top, 1)
                dve.wait_ge(top, done + 3)
                dve.tensor_reduce(pm_[:, :], pr_[:, :, :], AX.X, ALU.max).then_inc(top, 1)

            def route(it, part):
                n, m, i = it

                def bc(a):
                    return a[:, :, None].to_broadcast([Q, TU, NE])

                def flat(a):
                    return a[:, :, :].rearrange("p g e -> p (g e)")
                if part < 2:
                    tiles = slice(G * part, G * (part + 1))
                    parts = lg_ps(n, part).rearrange("p (g a e) -> p g a e", g=G, a=2)
                    dve.wait_ge(lgp_ok, 2 * n + part + 1)
                    dve.tensor_tensor(lg_hi[:, tiles, :], parts[:, :, 0, :],
                                      br_eff[:, None, :].to_broadcast([Q, G, NE]), ALU.add).then_inc(top, 1)
                    dve.wait_ge(top, TOP * n + 2 * part + 1)
                    dve.tensor_tensor(lg[:, tiles, :], parts[:, :, 1, :], lg_hi[:, tiles, :], ALU.add)\
                        .then_inc(top, 1)
                if part == 2:
                    dve.wait_ge(top, TOP * n + 4)
                    largest(TOP * n + 4, lg, top1, is1, pr1, pm1)
                if part == 3:
                    dve.wait_ge(top, TOP * n + 8)
                    dve.tensor_tensor(sel1[:, :, :], pr1[:, :, :], bc(pm1), ALU.is_equal).then_inc(top, 1)
                    dve.wait_ge(top, TOP * n + 9)
                    dve.scalar_tensor_tensor(out=flat(lg2), in0=flat(sel1), scalar=-3e38, in1=flat(lg),
                                             op0=ALU.mult, op1=ALU.add).then_inc(top, 1)
                    dve.wait_ge(top, TOP * n + 10)
                    largest(TOP * n + 10, lg2, top2, is2, pr2, pm2)
                    dve.tensor_tensor(gap[:, :], top1[:, :], top2[:, :], ALU.subtract).then_inc(top, 1)
                if part == 4:
                    dve.wait_ge(top, TOP * n + 15)
                    dve.tensor_tensor(sel2[:, :, :], pr2[:, :, :], bc(pm2), ALU.is_equal).then_inc(top, 1)
                if part == 5:
                    dve.wait_ge(tanh_ok, n + 1)
                    dve.tensor_scalar(wt1[:, :], tanh[:, :], 0.5, 0.5, ALU.mult, ALU.add).then_inc(top, 1)
                    dve.tensor_scalar(wt2[:, :], tanh[:, :], -0.5, 0.5, ALU.mult, ALU.add).then_inc(top, 1)
                    dve.wait_ge(top, TOP * n + 18)
                    dve.tensor_tensor(mix1[:, :, :], sel1[:, :, :], bc(wt1), ALU.mult).then_inc(top, 1)
                    dve.tensor_tensor(mix2[:, :, :], sel2[:, :, :], bc(wt2), ALU.mult).then_inc(top, 1)
                    dve.wait_ge(top, TOP * n + 20)
                    dve.tensor_tensor(mix[:, :, :], mix1[:, :, :], mix2[:, :, :], ALU.add).then_inc(top, 1)
                    dve.wait_ge(top, TOP * n + 21)
                    if not first(n):
                        dve.wait_ge(mTp_ok, n)
                    for c in range(2):
                        last = dve.tensor_copy(msplit[:, :, 0, c, :], mix[:, G * c:G * (c + 1), :])
                    last.then_inc(top, 1)
                    dve.wait_ge(top, TOP * n + 22)
                    for c in range(2):
                        last = dve.tensor_tensor(msplit[:, :, 1, c, :], mix[:, G * c:G * (c + 1), :],
                                                 msplit[:, :, 0, c, :], ALU.subtract)
                    last.then_inc(top, 1)

            def step_b(half, j, experts=range(NE)):
                nxt, prep, main, fin = (item(half, j, lag, UNITS) for lag in range(4))
                for e in experts:
                    if main:
                        n, m, i = main
                        k = NE * n + e
                        dve.wait_ge(yp_ok, k + 1)
                        dve.wait_ge(mb_ok, k + 1)
                        if e == 0:
                            if not first(n, 2):
                                dve.wait_ge(backB_ok, n - 1)
                        elif not first(n) or e > 2:
                            dve.wait_ge(acc_ok, (NE - 1) * n + max(e - 2, 0))
                        dst = ye[e % 2] if e else acc[i]
                        dve.scalar_tensor_tensor(out=dst[:, :], in0=y_ps[e % 2][:, 0:C], scalar=b2_col[:, e:e + 1],
                                                 in1=mb[e % 2][:, :], op0=ALU.add, op1=ALU.mult).then_inc(ye_ok, 1)
                    if prep and e == 1:
                        route(prep, 0)
                    if nxt and e < 2:
                        norm(nxt, e)
                    if prep and e == 2:
                        route(prep, 1)
                        route(prep, 2)
                    if prep and e == 3:
                        route(prep, 3)
                    if nxt and e == 4:
                        norm(nxt, 2)
                    if prep and e == 4:
                        route(prep, 4)
                    if prep and e == 5:
                        route(prep, 5)
                    if fin and e == 6:
                        n, m, i = fin
                        dve.wait_ge(backB_ok, n + 1)
                        moe = aux_ps[0:Q, :].rearrange("p (g c d) -> p c g d", g=G, c=2)
                        for c in range(2):
                            last = dve.tensor_tensor(
                                y[:, bass.ds(2 * n + c, 1), :, :].rearrange("p a g d -> p (a g) d"), moe[:, c],
                                H1[:, bass.ds(2 * n + c, 1), :].rearrange("p a (g d) -> p (a g) d", d=D), ALU.add)
                        last.then_inc(y_ok, 1)

            run(dve, step_a, step_b, EARLY_B_VECTOR)


POOL_PREP = 8 + 4 + 1 + 2
ACT_PREP = 9
DVE_PREP = 9

_INS = ['x', 'L0_tok_w', 'L0_tok_b', 'L0_attn_Wq', 'L0_attn_bq', 'L0_attn_Wk', 'L0_attn_bk', 'L0_attn_Wv',
        'L0_attn_bv', 'L0_attn_Wo', 'L0_attn_bo', 'L0_ffn_gamma', 'L0_ffn_beta', 'L0_ffn_Wr', 'L0_ffn_br',
        'L0_ffn_W1', 'L0_ffn_b1', 'L0_ffn_W2', 'L0_ffn_b2']
KEPT = 0.8


def kernel(**inputs):
    import numpy as _np
    import concourse.bacc as _bacc
    from concourse import mybir as _mybir
    from concourse.bass_utils import run_bass_kernel_spmd as _run

    nc = _bacc.Bacc("TRN2", target_bir_lowering=False, num_devices=1)
    arrays, args = {}, []
    for name in _INS:
        a = _np.ascontiguousarray(inputs[name])
        arrays[f"in_{name}"] = a
        args.append(nc.dram_tensor(f"in_{name}", a.shape, _mybir.dt.from_np(a.dtype), kind="ExternalInput").ap())
    b, n, d = inputs['x'].shape
    args.append(nc.dram_tensor("out_0", (b, max(1, int(n * KEPT)), d), _mybir.dt.float32, kind="ExternalOutput").ap())
    audio_tower_kernel(nc, *args)
    r = _run(nc, [arrays], core_ids=[0])
    return r.results[0]["out_0"]
```
